# Optimizing a Trainium2 kernel written in Bass

```python
import numpy as np
import jax
import jax.numpy as jnp

def _softmax(x, axis=-1):
    return jax.nn.softmax(x, axis=axis)

def _gelu(x):
    return jax.nn.gelu(x, approximate=True)

def _silu(x):
    return jax.nn.silu(x)

def _sigmoid(x):
    return jax.nn.sigmoid(x)

def _layernorm(x, axis=-1, eps=1e-05):
    m = jnp.mean(x, axis=axis, keepdims=True)
    v = jnp.var(x, axis=axis, keepdims=True)
    return (x - m) / jnp.sqrt(v + eps)

def _scatter_add(tgt, idx, src, axis=0):
    return tgt.at[idx].add(src)

def _segment_sum(src, seg, n):
    return jax.ops.segment_sum(src, seg, n)
kernel_name = 'mk_seq_postln_d1_jaxref_r8_49c300'

def setup_inputs(seed: int=0):
    np.random.seed(seed)
    _w = jnp.asarray

    def _L0_attn_setup():
        import math
        import jax, jax.numpy as jnp
        import numpy as np
        D_MODEL = 128
        NUM_HEADS = 16
        HEAD_DIM = D_MODEL // NUM_HEADS
        B, T = (4, 256)

        def _get_slopes(n_heads: int) -> np.ndarray:

            def pow2_slopes(n):
                start = 2 ** (-2 ** (-(math.log2(n) - 3)))
                return [start * start ** i for i in range(n)]
            if math.log2(n_heads).is_integer():
                return np.array(pow2_slopes(n_heads), dtype=np.float32)
            closest = 2 ** math.floor(math.log2(n_heads))
            slopes = pow2_slopes(closest)
            slopes += pow2_slopes(2 * closest)[0::2][:n_heads - closest]
            return np.array(slopes[:n_heads], dtype=np.float32)
        key = jax.random.key(seed)
        ks = jax.random.split(key, 6)
        init = 0.02
        return {'x': jax.random.normal(ks[0], (B, T, D_MODEL), dtype=jnp.float32), 'wq': jax.random.normal(ks[1], (D_MODEL, D_MODEL), dtype=jnp.float32) * init, 'wk': jax.random.normal(ks[2], (D_MODEL, D_MODEL), dtype=jnp.float32) * init, 'wv': jax.random.normal(ks[3], (D_MODEL, D_MODEL), dtype=jnp.float32) * init, 'wo': jax.random.normal(ks[4], (D_MODEL, D_MODEL), dtype=jnp.float32) * init, 'bo': jnp.zeros((D_MODEL,), dtype=jnp.float32)}
    _L0_attn_in = _L0_attn_setup()

    def _L0_ffn_setup():
        import jax, jax.numpy as jnp
        import numpy as np
        D_IN, D_HID = (128, 512)

        def _ternary(key, shape):
            return jax.random.randint(key, shape, -1, 2).astype(jnp.float32)

        def _tlin(x, w, s):
            return jnp.einsum('bsi,oi->bso', x, w) * s
        key = jax.random.key(seed)
        ks = jax.random.split(key, 12)
        inv = lambda fan: 1.0 / np.sqrt(fan).astype(np.float32)
        return {'x': jax.random.normal(ks[0], (4, 256, D_IN), dtype=jnp.float32), 'w1_w': _ternary(ks[1], (D_HID, D_IN)), 'w1_s': jax.random.uniform(ks[2], (D_HID,), dtype=jnp.float32) * inv(D_IN), 'w2_w': _ternary(ks[3], (D_HID, D_IN)), 'w2_s': jax.random.uniform(ks[4], (D_HID,), dtype=jnp.float32) * inv(D_IN), 'h1_w': _ternary(ks[5], (D_HID, D_HID)), 'h1_s': jax.random.uniform(ks[6], (D_HID,), dtype=jnp.float32) * inv(D_HID), 'h2_w': _ternary(ks[7], (D_HID, D_HID)), 'h2_s': jax.random.uniform(ks[8], (D_HID,), dtype=jnp.float32) * inv(D_HID), 'w3_w': _ternary(ks[9], (D_IN, D_HID)), 'w3_s': jax.random.uniform(ks[10], (D_IN,), dtype=jnp.float32) * inv(D_HID)}
    _L0_ffn_in = _L0_ffn_setup()
    _d = {'L0_attn_x': _L0_attn_in['x'], 'L0_attn_wq': _L0_attn_in['wq'], 'L0_attn_wk': _L0_attn_in['wk'], 'L0_attn_wv': _L0_attn_in['wv'], 'L0_attn_wo': _L0_attn_in['wo'], 'L0_attn_bo': _L0_attn_in['bo'], 'L0_ffn_w1_w': _L0_ffn_in['w1_w'], 'L0_ffn_w1_s': _L0_ffn_in['w1_s'], 'L0_ffn_w2_w': _L0_ffn_in['w2_w'], 'L0_ffn_w2_s': _L0_ffn_in['w2_s'], 'L0_ffn_h1_w': _L0_ffn_in['h1_w'], 'L0_ffn_h1_s': _L0_ffn_in['h1_s'], 'L0_ffn_h2_w': _L0_ffn_in['h2_w'], 'L0_ffn_h2_s': _L0_ffn_in['h2_s'], 'L0_ffn_w3_w': _L0_ffn_in['w3_w'], 'L0_ffn_w3_s': _L0_ffn_in['w3_s']}
    _x0 = _d['L0_attn_x']
    _d['L0_attn_x'] = jax.random.normal(jax.random.fold_in(jax.random.key(seed), 1), (32, 256, 128), dtype=_x0.dtype)
    del _x0
    return _d

def reference(L0_attn_x, L0_attn_wq, L0_attn_wk, L0_attn_wv, L0_attn_wo, L0_attn_bo, L0_ffn_w1_w, L0_ffn_w1_s, L0_ffn_w2_w, L0_ffn_w2_s, L0_ffn_h1_w, L0_ffn_h1_s, L0_ffn_h2_w, L0_ffn_h2_s, L0_ffn_w3_w, L0_ffn_w3_s):

    def _L0_attn_ref(x, wq, wk, wv, wo, bo):
        import math
        import jax, jax.numpy as jnp
        import numpy as np
        D_MODEL = 128
        NUM_HEADS = 16
        HEAD_DIM = D_MODEL // NUM_HEADS
        B, T = (4, 256)

        def _get_slopes(n_heads: int) -> np.ndarray:

            def pow2_slopes(n):
                start = 2 ** (-2 ** (-(math.log2(n) - 3)))
                return [start * start ** i for i in range(n)]
            if math.log2(n_heads).is_integer():
                return np.array(pow2_slopes(n_heads), dtype=np.float32)
            closest = 2 ** math.floor(math.log2(n_heads))
            slopes = pow2_slopes(closest)
            slopes += pow2_slopes(2 * closest)[0::2][:n_heads - closest]
            return np.array(slopes[:n_heads], dtype=np.float32)
        Bx, Tx, _ = x.shape
        H, Dh = (NUM_HEADS, HEAD_DIM)
        scale = math.sqrt(Dh)
        q = (x @ wq.T).reshape(Bx, Tx, H, Dh).transpose(0, 2, 1, 3)
        k = (x @ wk.T).reshape(Bx, Tx, H, Dh).transpose(0, 2, 1, 3)
        v = (x @ wv.T).reshape(Bx, Tx, H, Dh).transpose(0, 2, 1, 3)
        attn = jnp.einsum('bhqd,bhkd->bhqk', q, k) / scale
        pos = jnp.arange(Tx)
        dist = -jnp.abs(pos[None, :] - pos[:, None]).astype(jnp.float32)
        slopes = jnp.asarray(_get_slopes(H))
        attn = attn + slopes[None, :, None, None] * dist[None, None, :, :]
        attn = jax.nn.softmax(attn, axis=-1)
        out = jnp.einsum('bhqk,bhkd->bhqd', attn, v)
        out = out.transpose(0, 2, 1, 3).reshape(Bx, Tx, H * Dh)
        return out @ wo.T + bo

    def _L0_ffn_ref(x, w1_w, w1_s, w2_w, w2_s, h1_w, h1_s, h2_w, h2_s, w3_w, w3_s):
        import jax, jax.numpy as jnp
        import numpy as np
        D_IN, D_HID = (128, 512)

        def _ternary(key, shape):
            return jax.random.randint(key, shape, -1, 2).astype(jnp.float32)

        def _tlin(x, w, s):
            return jnp.einsum('bsi,oi->bso', x, w) * s
        h = jax.nn.silu(_tlin(x, w1_w, w1_s)) * _tlin(x, w2_w, w2_s)
        h = jax.nn.gelu(_tlin(h, h1_w, h1_s), approximate=False)
        h = jax.nn.gelu(_tlin(h, h2_w, h2_s), approximate=False)
        return _tlin(h, w3_w, w3_s)
    x = L0_attn_x
    x = _layernorm(x + _L0_attn_ref(x, L0_attn_wq, L0_attn_wk, L0_attn_wv, L0_attn_wo, L0_attn_bo), axis=-1)
    x = _layernorm(x + _L0_ffn_ref(x, L0_ffn_w1_w, L0_ffn_w1_s, L0_ffn_w2_w, L0_ffn_w2_s, L0_ffn_h1_w, L0_ffn_h1_s, L0_ffn_h2_w, L0_ffn_h2_s, L0_ffn_w3_w, L0_ffn_w3_s), axis=-1)
    return x

_drawn_inputs = setup_inputs


def setup_inputs(seed=0):
    import zlib

    import numpy as np

    out = dict(_drawn_inputs(seed))
    spreads = {'L0_attn_bo': (0.0, 0.1)}
    factors = {'L0_attn_wq': 8.0,
     'L0_attn_wk': 8.0,
     'L0_attn_wv': 5.463,
     'L0_attn_wo': 5.554,
     'L0_ffn_w1_w': 8.0,
     'L0_ffn_w1_s': 8.0,
     'L0_ffn_w2_w': 8.0,
     'L0_ffn_w2_s': 8.0,
     'L0_ffn_h1_w': 8.0,
     'L0_ffn_h1_s': 8.0,
     'L0_ffn_h2_w': 8.0,
     'L0_ffn_h2_s': 8.0,
     'L0_ffn_w3_w': 8.0,
     'L0_ffn_w3_s': 8.0}
    for name, (base, spread) in spreads.items():
        noise = np.random.default_rng([zlib.crc32(name.encode()), seed]).standard_normal(out[name].shape)
        drawn = base * np.exp(spread * noise) if base else spread * noise
        out[name] = jnp.asarray(drawn.astype(out[name].dtype))
    for name, factor in factors.items():
        out[name] = (out[name] * factor).astype(out[name].dtype)
    return out
```

```python
from contextlib import ExitStack

import numpy as np

import concourse.bass as bass
from concourse import mybir

F32 = mybir.dt.float32
F32R = mybir.dt.float32r
BF16 = mybir.dt.bfloat16
ACT = mybir.ActivationFunctionType
ALU = mybir.AluOpType
AX_X = mybir.AxisListType.X

P = 128
BATCH = 32
SEQ = 256
D = 128
HEADS = 16
DH = D // HEADS
BLK = SEQ // P
HALF = HEADS // 2
GROUP = 4
VCOLS = 32
HID = 512
KT = HID // P
CHUNK = 512
CB = CHUNK // P
CHUNKS = BATCH * SEQ // CHUNK
EPS = 1e-5
DMA = 16

STACK = 3 * DH
BIAS = STACK
KA = 96
MROW = 96
QH, QL, KH, KL = range(4)


def slopes():
    start = 2.0 ** (-2.0 ** (-(np.log2(HEADS) - 3)))
    return [float(np.float32(start * start ** i)) for i in range(HEADS)]


def runs(n_or_value):
    return not isinstance(n_or_value, int) or n_or_value > 0


def wait(eng, sem, value):
    if runs(value):
        eng.wait_ge(sem, value)


def wait_apart(eng, sem, value, passed):
    wait(eng, sem, value)
    if not isinstance(value, int):
        eng.sem_inc(passed, 1)


def live(index, count):
    return not isinstance(index, int) or 0 <= index < count


def drive(eng, step, first, loop_from, loop_to, last, unroll):
    for t in range(first, loop_from):
        step(t, t % 2)
    with eng.Fori(0, (loop_to - loop_from) // unroll, 1) as i:
        for u in range(unroll):
            step(i * unroll + (loop_from + u), (loop_from + u) % 2)
    for t in range(loop_to, last + 1):
        step(t, t % 2)


def attention(nc, wts, x, xT, wqT, wkT, wvT, woT, bo, qscale, ident, tri, rows, x1_dram, qk_dram, raw_w):
    slope = slopes()
    with ExitStack() as ctx:
        def sb(name, shape, dt=F32):
            return ctx.enter_context(nc.sbuf_tensor(name, shape, dt))

        def sem(name):
            return ctx.enter_context(nc.semaphore(name))

        wq_sb, wk_sb, wv_sb, wo_sb = (sb(n, [P, D]) for n in ("wq_sb", "wk_sb", "wv_sb", "wo_sb"))
        bo_sb = sb("bo_sb", [P, D])
        qscale_sb = sb("qscale_sb", [P, 1])
        id_sb = sb("id_sb", [P, P])
        idb_sb = sb("idb_sb", [P, P], BF16)
        tri_f = sb("tri_f", [P, 2, P])
        tri_sb = sb("tri_sb", [P, 2, P], BF16)
        trir_sb = sb("trir_sb", [P, 2, P], BF16)
        minus_half = sb("minus_half", [P, BLK])
        q_stack = [sb(f"q_stack{i}", [P, HEADS, SEQ], F32R) for i in range(2)]
        k_stack = [sb(f"k_stack{i}", [P, HEADS, SEQ], F32R) for i in range(2)]
        probs = sb("probs", [P, HALF, BLK * SEQ])
        v_aug = [sb(f"v_aug{i}", [P, BLK, HEADS, VCOLS]) for i in range(2)]
        xT_sb = [sb(f"xT_sb{i}", [P, SEQ]) for i in range(2)]
        qk_sb = sb("qk_sb", [P, 4, SEQ], F32R)
        x_sb = [sb(f"x_sb{i}", [P, BLK, D]) for i in range(2)]
        xb_sb = [sb(f"xb_sb{i}", [P, BLK, D]) for i in range(2)]
        negmax = sb("negmax", [P, 2, BLK, HALF])
        mrow_hi = [sb(f"mrow_hi{i}", [BLK * HALF, P], F32R) for i in range(2)]
        mrow_lo = [sb(f"mrow_lo{i}", [BLK * HALF, P], F32R) for i in range(2)]
        o_sb = sb("o_sb", [P, HEADS // GROUP, SEQ])
        recip = sb("recip", [P, BLK, HEADS])
        o_norm = sb("o_norm", [P, BLK, D])
        oT_sb = sb("oT_sb", [P, SEQ])
        res = [sb(f"res{i}", [P, BLK, D]) for i in range(2)]
        bn6 = sb("bn6", [P, BLK, 6])
        meanvar = [sb(f"meanvar{i}", [P, BLK, 2]) for i in range(2)]
        vareps = sb("vareps", [P, BLK])
        rstd = sb("rstd", [P, BLK])
        x1_sb = [sb(f"x1_sb{i}", [P, BLK, D]) for i in range(2)]
        raw = sb("raw", [P, 2, 2, HID])

        ps_a = [ctx.enter_context(nc.psum_tensor(f"ps_a{i}", [P, 512], F32)) for i in range(2)]
        ps_b = [ctx.enter_context(nc.psum_tensor(f"ps_b{i}", [P, 512], F32)) for i in range(2)]
        ps_o = [ctx.enter_context(nc.psum_tensor(f"ps_o{i}", [P, 512], F32)) for i in range(2)]
        ps_m = [ctx.enter_context(nc.psum_tensor(f"ps_m{i}", [P, 512], F32)) for i in range(2)]

        passed = {e: sem(f"passed_{e}") for e in ("sp", "dve", "pool")}
        const_landed = sem("const_landed")
        const_set = sem("const_set")
        ones_landed = sem("ones_landed")
        xT_landed, x_landed = sem("xT_landed"), sem("x_landed")
        qk_done, qk_hi, qk_lo = sem("qk_done"), sem("qk_hi"), sem("qk_lo")
        spilled = sem("spilled")
        stacked = [sem(f"stacked{i}") for i in range(2)]
        v_done, v_copied = sem("v_done"), sem("v_copied")
        scores_a, max_done = sem("scores_a"), sem("max_done")
        mT_done, m_hi, m_lo = sem("mT_done"), sem("m_hi"), sem("m_lo")
        m_landed = [sem(f"m_landed{i}") for i in range(2)]
        scores_b, exp_done = sem("scores_b"), sem("exp_done")
        pv_done, o_copied = sem("pv_done"), sem("o_copied")
        o_turned, recip_done, normed = sem("o_turned"), sem("recip_done"), sem("normed")
        oT_done, oT_copied = sem("oT_done"), sem("oT_copied")
        wo_done, res_done = sem("wo_done"), sem("res_done")
        bn_done, stats_done = sem("bn_done"), sem("stats_done")
        eps_done, rstd_done = sem("eps_done"), sem("rstd_done")
        xb_done, x1_done, x1_stored = sem("xb_done"), sem("x1_done"), sem("x1_stored")
        raw_landed, raw_split = [sem(f"raw_landed{i}") for i in range(2)], sem("raw_split")
        raw_hi = sem("raw_hi")

        pieces = []
        for (hi, lo), src in zip(wts, raw_w):
            kt = hi.shape[1]
            for a in range(0, kt, 2):
                pieces.append((hi[:, a:min(a + 2, kt), :], lo[:, a:min(a + 2, kt), :],
                               src[:, a:min(a + 2, kt), :]))
        piece_step = [-2, -1, -1, 0, 29, 29, 30, 30, 31, 31, 32][:len(pieces)]
        assert len(pieces) <= 11
        N_CONST = 9
        N_SPLIT = 3 * 2
        STEPS = dict(first=-2, loop_from=3, loop_to=BATCH - 3, last=BATCH, unroll=2)
        FIRST = STEPS["first"]

        block = ctx.enter_context(nc.Block())

        @block.sync
        def _(sp):
            sp.dma_start(xT_sb[0][:], xT[0]).then_inc(xT_landed, DMA)
            for dst, src in ((wq_sb, wqT), (wk_sb, wkT), (wv_sb, wvT), (wo_sb, woT), (bo_sb, bo), (id_sb, ident),
                             (qscale_sb, qscale)):
                sp.dma_start(dst[:], src).then_inc(const_landed, DMA)
            for a in range(2):
                sp.dma_start(tri_f[:, a, :], tri[a]).then_inc(const_landed, DMA)
            sp.dma_start(probs[0:4, :, :].rearrange("p a b -> p (a b)"), rows).then_inc(ones_landed, DMA)
            sp.wait_ge(xT_landed, DMA)
            sp.dma_start(xT_sb[1][:], xT[1]).then_inc(xT_landed, DMA)
            sp.dma_start(x_sb[0][:], x[0].rearrange("(a p) d -> p a d", p=P)).then_inc(x_landed, DMA)
            sp.wait_ge(ones_landed, DMA)
            sp.wait_ge(const_set, 4)
            flat = probs[0:4, :, :].rearrange("p a b -> p (a b)")
            for i in range(2):
                for dst, r0 in ((q_stack[i][BIAS:BIAS + 2, :, :], 0), (k_stack[i][BIAS:BIAS + 2, :, :], 2),
                                (k_stack[i][MROW:MROW + 1, :, :], 2), (k_stack[i][MROW + 1:MROW + 2, :, :], 2)):
                    n = dst.shape[0]
                    sp.dma_start(dst.bitcast(F32).rearrange("p h t -> p (h t)"), flat[r0:r0 + n, :]).then_inc(ones_landed, DMA)
            for n in range(2):
                d = pieces[n][2]
                sp.dma_start(raw[:, n, 0:d.shape[1], 0:d.shape[2]], d).then_inc(raw_landed[n], DMA)

            def stack(b, par, hf):
                heads = slice(hf * HALF, (hf + 1) * HALF)
                for dst, parts in ((q_stack[par], (QH, QH, QL)), (k_stack[par], (KH, KL, KH))):
                    for r, part in enumerate(parts):
                        src = qk_dram[par, hf * 64:(hf + 1) * 64, part, :].rearrange("(h d) t -> d h t", d=DH)
                        sp.dma_start(dst[r * DH:(r + 1) * DH, heads, :].bitcast(F32), src).then_inc(stacked[hf], DMA)

            def max_rows(b, par, hf):
                wait_apart(sp, m_lo, b * 2 + hf + 1, passed["sp"])
                for r, src in enumerate((mrow_hi[hf], mrow_lo[hf])):
                    for qb in range(BLK):
                        dst = q_stack[par][MROW + r:MROW + r + 1, hf * HALF:(hf + 1) * HALF, qb * P:(qb + 1) * P]
                        sp.dma_start(dst.bitcast(F32), src[qb * HALF:(qb + 1) * HALF, :].bitcast(F32)).then_inc(m_landed[hf], DMA)

            def step(t, s):
                if live(t + 1, BATCH):
                    wait_apart(sp, spilled, (t + 2) * DMA, passed["sp"])
                    wait_apart(sp, scores_b, t * HEADS, passed["sp"])
                    stack(t + 1, 1 - s, 1)
                if live(t, BATCH):
                    max_rows(t, s, 1)
                if live(t - 2, BATCH):
                    wait_apart(sp, x1_done, t - 1, passed["sp"])
                    wait_apart(sp, x1_stored, (t - 2) * DMA, passed["sp"])
                    sp.dma_start(x1_dram[t - 2], x1_sb[s][:]).then_inc(x1_stored, DMA)
                if live(t + 3, BATCH) and live(t + 1, BATCH):
                    wait_apart(sp, v_done, t + 2, passed["sp"])
                    wait_apart(sp, xT_landed, (t + 3) * DMA, passed["sp"])
                    sp.dma_start(xT_sb[1 - s][:], xT[t + 3]).then_inc(xT_landed, DMA)
                if live(t + 1, BATCH) and live(t, BATCH):
                    wait_apart(sp, xb_done, t, passed["sp"])
                    wait_apart(sp, x_landed, (t + 1) * DMA, passed["sp"])
                    sp.dma_start(x_sb[1 - s][:], x[t + 1].rearrange("(a p) d -> p a d", p=P)).then_inc(x_landed, DMA)
                if live(t + 2, BATCH):
                    wait_apart(sp, qk_lo, (t + 2) * 2 + 2, passed["sp"])
                    if live(t, BATCH):
                        wait_apart(sp, stacked[0], (t + 1) * N_SPLIT * DMA, passed["sp"])
                        wait_apart(sp, stacked[1], (t + 1) * N_SPLIT * DMA, passed["sp"])
                    sp.dma_start(qk_dram[s], qk_sb[:].bitcast(F32)).then_inc(spilled, DMA)
                    wait_apart(sp, spilled, (t + 3) * DMA, passed["sp"])
                    if live(t, BATCH):
                        wait_apart(sp, scores_b, t * HEADS + HALF, passed["sp"])
                    else:
                        sp.wait_ge(const_set, 4)
                    stack(t + 2, s, 0)
                if live(t + 1, BATCH):
                    max_rows(t + 1, 1 - s, 0)
                if isinstance(t, int):
                    for n, at in enumerate(piece_step):
                        if at == t and n + 2 < len(pieces):
                            sp.wait_ge(raw_split, n + 1)
                            d = pieces[n + 2][2]
                            sp.dma_start(raw[:, n % 2, 0:d.shape[1], 0:d.shape[2]], d).then_inc(raw_landed[n % 2], DMA)

            drive(sp, step, **STEPS)
            sp.wait_ge(x1_done, BATCH)
            sp.wait_ge(x1_stored, (BATCH - 1) * DMA)
            sp.dma_start(x1_dram[BATCH - 1], x1_sb[(BATCH - 1) % 2][:]).then_inc(x1_stored, DMA)
            sp.wait_ge(x1_stored, BATCH * DMA)

        @block.tensor
        def _(pe):
            def add_bias(ps, table):
                out = ps[:].rearrange("p (b c) -> p b c", c=P)[:, 0:4:3, :]
                return pe.matmul(out, idb_sb[:], table[:], start=False, stop=True, skip_group_check=True)

            def score_max(b, par, h):
                if h % HALF == 0:
                    wait(pe, stacked[h // HALF], (b + 1) * N_SPLIT * DMA)
                wait(pe, max_done, b * HEADS + h - 1)
                ps = ps_a[h % 2]
                for qb in range(BLK):
                    pe.matmul(ps[:, qb * SEQ:(qb + 1) * SEQ], q_stack[par][0:KA, h, qb * P:(qb + 1) * P],
                              k_stack[par][0:KA, h, :], start=(qb == 0), stop=False, skip_group_check=True)
                add_bias(ps, tri_sb).then_inc(scores_a, 1)

            def score_exp(b, par, h):
                if h % HALF == 0:
                    wait(pe, m_landed[h // HALF], (b + 1) * 4 * DMA)
                wait(pe, exp_done, b * HEADS + h - 1)
                ps = ps_b[h % 2]
                for kb in range(BLK):
                    pe.matmul(ps[:, kb * SEQ:(kb + 1) * SEQ], k_stack[par][:, h, kb * P:(kb + 1) * P],
                              q_stack[par][:, h, :], start=(kb == 0), stop=False, skip_group_check=True)
                add_bias(ps, trir_sb).then_inc(scores_b, 1)

            def pv(b, par, j):
                if j == 0:
                    wait(pe, v_copied, b + 1)
                wait(pe, exp_done, b * HEADS + GROUP * (j + 1))
                if j % 2 == 0:
                    wait(pe, o_copied, b * 2 + j // 2 - 1)
                for kb in range(BLK):
                    for g in range(GROUP):
                        h = j * GROUP + g
                        mm = pe.matmul(ps_o[j // 2][VCOLS * g:VCOLS * (g + 1), (j % 2) * SEQ:(j % 2 + 1) * SEQ],
                                       v_aug[par][:, kb, h, :], probs[:, h % HALF, kb * SEQ:(kb + 1) * SEQ],
                                       start=(kb == 0), stop=(kb == BLK - 1), skip_group_check=True)
                mm.then_inc(pv_done, 1)

            def turn_max(b, hf):
                wait(pe, max_done, b * HEADS + (hf + 1) * HALF)
                pe.transpose(ps_m[0][0:BLK * HALF, 0:P], negmax[:, hf, :, :].rearrange("p a h -> p (a h)"),
                             id_sb[:]).then_inc(mT_done, 1)

            def turn_o(b, qb):
                wait(pe, o_copied, b * 2 + 2)
                for j in range(HEADS // GROUP):
                    mm = pe.transpose(ps_m[qb][:, j * P:(j + 1) * P], o_sb[:, j, qb * P:(qb + 1) * P], id_sb[:])
                mm.then_inc(o_turned, 1)

            def step(t, s):
                for k in range(HEADS):
                    if live(t + 1, BATCH):
                        score_max(t + 1, 1 - s, k)
                    if live(t, BATCH):
                        score_exp(t, s, k)
                        if k >= 5 and k % GROUP == 1:
                            pv(t, s, k // GROUP - 1)
                    if k == 1 and live(t - 1, BATCH):
                        pv(t - 1, 1 - s, 3)
                    if k == 1 and live(t, BATCH):
                        wait(pe, m_lo, t * 2 + 1)
                        turn_max(t, 1)
                    if k == 2 and live(t + 1, BATCH):
                        wait(pe, xT_landed, (t + 2) * DMA)
                        if live(t - 2, BATCH):
                            wait(pe, res_done, t - 1)
                        elif live(t, BATCH):
                            wait(pe, v_copied, t + 1)
                        for tb in range(BLK):
                            mm = pe.matmul(ps_m[1][:, tb * D:(tb + 1) * D], xT_sb[1 - s][:, tb * P:(tb + 1) * P], wv_sb[:],
                                           start=True, stop=True)
                        mm.then_inc(v_done, 1)
                    if k == 4 and live(t - 1, BATCH):
                        if live(t, BATCH):
                            wait(pe, m_lo, t * 2 + 2)
                        else:
                            wait(pe, normed, (t - 2) * 2 + 1)
                        turn_o(t - 1, 0)
                    if k == 5 and live(t - 1, BATCH):
                        if live(t + 1, BATCH):
                            wait(pe, v_copied, t + 2)
                        else:
                            wait(pe, res_done, t - 1)
                        turn_o(t - 1, 1)
                    if k == 6 and live(t + 2, BATCH):
                        wait(pe, xT_landed, (t + 3) * DMA)
                        if live(t - 1, BATCH):
                            wait(pe, normed, (t - 1) * 2 + 1)
                        elif live(t, BATCH):
                            wait(pe, m_lo, t * 2 + 2)
                        else:
                            wait(pe, qk_lo, (t + 1) * 2 + 2)
                        if isinstance(t, int) and t == FIRST:
                            pe.wait_ge(const_landed, N_CONST * DMA)
                            pe.wait_ge(const_set, 12)
                        for n, w in enumerate((wq_sb, wk_sb)):
                            mm = pe.matmul(ps_m[0][:, n * SEQ:(n + 1) * SEQ], w[:], xT_sb[s][:], start=True, stop=True)
                        mm.then_inc(qk_done, 1)
                    if k == 8 and live(t - 1, BATCH):
                        wait(pe, normed, (t - 1) * 2 + 2)
                        for qb in range(BLK):
                            mm = pe.transpose(ps_m[1][:, qb * P:(qb + 1) * P], o_norm[:, qb, :], id_sb[:])
                        mm.then_inc(oT_done, 1)
                    if k == 9 and live(t + 1, BATCH):
                        if live(t + 2, BATCH):
                            wait(pe, qk_lo, (t + 2) * 2 + 2)
                        else:
                            wait(pe, normed, (t - 1) * 2 + 1)
                        turn_max(t + 1, 0)
                    if k == 11 and live(t - 1, BATCH):
                        wait(pe, oT_copied, t)
                        for qb in range(BLK):
                            mm = pe.matmul(ps_m[1][:, qb * D:(qb + 1) * D], oT_sb[:, qb * P:(qb + 1) * P], wo_sb[:],
                                           start=True, stop=True)
                        mm.then_inc(wo_done, 1)

            drive(pe, step, **STEPS)

        @block.scalar
        def _(act):
            def max_hi(b, hf):
                wait(act, mT_done, b * 2 + hf + 1)
                wait(act, m_landed[hf], b * 4 * DMA)
                nc.scalar.activation(mrow_hi[hf][:], ps_m[0][0:BLK * HALF, 0:P], ACT.Copy).then_inc(m_hi, 1)

            def copy_o(b, hf):
                wait(act, pv_done, b * 4 + hf * 2 + 2)
                wait(act, o_turned, b * 2)
                nc.scalar.activation(o_sb[:, 2 * hf:2 * hf + 2, :].rearrange("p j t -> p (j t)"), ps_o[hf][:],
                                     ACT.Copy).then_inc(o_copied, 1)

            def step(t, s):
                for k in range(HEADS):
                    if live(t, BATCH):
                        wait(act, scores_b, t * HEADS + k + 1)
                        if k % GROUP == 0:
                            wait(act, pv_done, t * 4 + k // GROUP - 1)
                        nc.scalar.activation(probs[:, k % HALF, :], ps_b[k % 2][:], ACT.Exp,
                                             scale=slope[k]).then_inc(exp_done, 1)
                    if k == 1 and live(t, BATCH):
                        max_hi(t, 1)
                    if k == 2 and live(t - 1, BATCH):
                        copy_o(t - 1, 1)
                    if k == 3 and live(t + 1, BATCH):
                        wait(act, v_done, t + 2)
                        wait(act, pv_done, t * 4)
                        if isinstance(t, int) and t < 1:
                            act.wait_ge(const_set, 8)
                        nc.scalar.activation(v_aug[1 - s][:, :, :, 0:DH],
                                             ps_m[1][:, 0:BLK * D].rearrange("p (a h d) -> p a h d", a=BLK, d=DH),
                                             ACT.Copy).then_inc(v_copied, 1)
                    if k == 7 and live(t + 2, BATCH):
                        wait(act, qk_done, t + 3)
                        wait(act, spilled, (t + 2) * DMA)
                        nc.scalar.activation(qk_sb[:, QH, :], ps_m[0][:, 0:SEQ], ACT.Copy,
                                             scale=qscale_sb[:, 0:1]).then_inc(qk_hi, 1)
                        nc.scalar.activation(qk_sb[:, KH, :], ps_m[0][:, SEQ:2 * SEQ], ACT.Copy).then_inc(qk_hi, 1)
                    if k == 9 and live(t - 1, BATCH):
                        wait(act, oT_done, t)
                        wait(act, wo_done, t - 1)
                        nc.scalar.activation(oT_sb[:], ps_m[1][:, 0:SEQ], ACT.Copy).then_inc(oT_copied, 1)
                    if k == 10 and live(t + 1, BATCH):
                        max_hi(t + 1, 0)
                    if k == 11 and live(t, BATCH):
                        copy_o(t, 0)

            act.wait_ge(const_landed, N_CONST * DMA)
            act.wait_ge(ones_landed, 9 * DMA)
            drive(act, step, **STEPS)

        @block.vector
        def _(dve):
            for i in range(2):
                nc.vector.memset(q_stack[i][:].bitcast(F32), 0.0).then_inc(const_set, 1)
                nc.vector.memset(k_stack[i][:].bitcast(F32), 0.0).then_inc(const_set, 1)
            for i in range(2):
                nc.vector.memset(v_aug[i][:, :, :, DH:VCOLS], 0.0).then_inc(const_set, 1)
            dve.wait_ge(const_set, 6)
            for i in range(2):
                nc.vector.memset(v_aug[i][:, :, :, DH:DH + 1], 1.0).then_inc(const_set, 1)
            dve.wait_ge(const_landed, N_CONST * DMA)
            nc.vector.tensor_copy(idb_sb[:], id_sb[:]).then_inc(const_set, 1)
            nc.vector.tensor_copy(tri_sb[:], tri_f[:]).then_inc(const_set, 1)
            for a in range(2):
                nc.vector.tensor_copy(trir_sb[:, a, :], tri_f[:, 1 - a, :]).then_inc(const_set, 1)

            def max_lo(b, hf):
                wait(dve, m_hi, b * 2 + hf + 1)
                nc.vector.tensor_tensor(mrow_lo[hf][:], ps_m[0][0:BLK * HALF, 0:P], mrow_hi[hf][:].bitcast(F32),
                                        ALU.subtract).then_inc(m_lo, 1)

            def normalise(b, qb):
                quad = ps_m[qb][:].rearrange("p (h c) -> p h c", c=VCOLS)
                wait(dve, o_turned, b * 2 + qb + 1)
                nc.vector.reciprocal(recip[:, qb, :], quad[:, :, DH]).then_inc(recip_done, 1)
                wait(dve, oT_done, b)
                wait(dve, recip_done, b * 2 + qb + 1)
                nc.vector.tensor_tensor(o_norm[:, qb, :].rearrange("p (h d) -> p h d", d=DH), quad[:, :, 0:DH],
                                        recip[:, qb, :].unsqueeze(2).broadcast_to([P, HEADS, DH]),
                                        ALU.mult).then_inc(normed, 1)

            def step(t, s):
                for k in range(HEADS):
                    if live(t + 1, BATCH):
                        wait(dve, scores_a, (t + 1) * HEADS + k + 1)
                        if k % HALF == 0:
                            wait(dve, mT_done, (t + 1) * 2 + k // HALF - 1)
                        nc.vector.tensor_reduce(negmax[:, k // HALF, :, k % HALF],
                                                ps_a[k % 2][:].rearrange("p (b c) -> p b c", b=BLK), AX_X, ALU.max,
                                                negate=True).then_inc(max_done, 1)
                    if k == 2 and live(t, BATCH):
                        max_lo(t, 1)
                    if k in (5, 6) and live(t - 1, BATCH):
                        normalise(t - 1, k - 5)
                    if k == 8 and live(t + 2, BATCH):
                        wait(dve, qk_hi, (t + 3) * 2)
                        nc.vector.scalar_tensor_tensor(
                            out=qk_sb[:, QL, :], in0=ps_m[0][:, 0:SEQ], scalar=qscale_sb[:, 0:1],
                            in1=qk_sb[:, QH, :].bitcast(F32), op0=ALU.mult, op1=ALU.subtract).then_inc(qk_lo, 1)
                        nc.vector.tensor_tensor(qk_sb[:, KL, :], ps_m[0][:, SEQ:2 * SEQ], qk_sb[:, KH, :].bitcast(F32),
                                                ALU.subtract).then_inc(qk_lo, 1)
                    if k == 11 and live(t + 1, BATCH):
                        max_lo(t + 1, 0)
                    if k == 12 and live(t - 1, BATCH):
                        wait(dve, wo_done, t)
                        wait(dve, xb_done, t)
                        wait(dve, x1_done, t - 2)
                        r = res[1 - s]
                        nc.vector.tensor_tensor(r[:].rearrange("p a d -> p (a d)"), ps_m[1][:, 0:BLK * D],
                                                xb_sb[1 - s][:].rearrange("p a d -> p (a d)"), ALU.add).then_inc(res_done, 1)
                        wait(dve, res_done, t)
                        for a in range(BLK):
                            nc.vector.bn_stats(bn6[:, a, :], r[:, a, :]).then_inc(bn_done, 1)
                        wait_apart(dve, bn_done, t * BLK, passed["dve"])
                        for a in range(BLK):
                            nc.vector.bn_aggr(meanvar[1 - s][:, a, :], bn6[:, a, :]).then_inc(stats_done, 1)

            drive(dve, step, **STEPS)

        @block.gpsimd
        def _(pool):
            nc.gpsimd.memset(minus_half[:], -0.5).then_inc(eps_done, 1)
            pool.wait_ge(const_landed, N_CONST * DMA)
            bo_b = bo_sb[:].unsqueeze(1).broadcast_to([P, BLK, D])

            def step(t, s):
                if live(t, BATCH):
                    wait(pool, x_landed, (t + 1) * DMA)
                    wait(pool, res_done, t - 1)
                    nc.gpsimd.tensor_tensor(xb_sb[s][:], x_sb[s][:], bo_b, ALU.add).then_inc(xb_done, 1)
                if live(t - 1, BATCH):
                    mv = meanvar[1 - s]
                    wait_apart(pool, stats_done, t * BLK, passed["pool"])
                    nc.gpsimd.tensor_scalar(vareps[:], mv[:, :, 1], EPS, None, ALU.add).then_inc(eps_done, 1)
                    wait(pool, eps_done, t + 1)
                    nc.gpsimd.tensor_tensor(rstd[:], vareps[:], minus_half[:], ALU.pow).then_inc(rstd_done, 1)
                    wait(pool, rstd_done, t)
                    wait_apart(pool, x1_stored, (t - 2) * DMA, passed["pool"])
                    for a in range(BLK):
                        ins = nc.gpsimd.tensor_scalar(x1_sb[1 - s][:, a, :], res[1 - s][:, a, :], mv[:, a, 0:1],
                                                      rstd[:, a:a + 1], ALU.subtract, ALU.mult)
                    ins.then_inc(x1_done, 1)
                if isinstance(t, int):
                    for n, at in enumerate(piece_step):
                        if at == t:
                            hi, lo, src = pieces[n]
                            w = raw[:, n % 2, 0:src.shape[1], 0:src.shape[2]]
                            pool.wait_ge(raw_landed[n % 2], (n // 2 + 1) * DMA)
                            nc.gpsimd.tensor_copy(hi, w).then_inc(raw_hi, 1)
                            pool.wait_ge(raw_hi, n + 1)
                            nc.gpsimd.tensor_tensor(lo, w, hi.bitcast(F32), ALU.subtract).then_inc(raw_split, 1)

            drive(pool, step, **STEPS)


def ffn(nc, wts, scales, ident, x1_dram, out):
    (w1h, w1l), (w2h, w2l), (h1h, h1l), (h2h, h2l), (w3h, w3l) = wts
    with ExitStack() as ctx:
        def sb(name, shape, dt=F32):
            return ctx.enter_context(nc.sbuf_tensor(name, shape, dt))

        def sem(name):
            return ctx.enter_context(nc.semaphore(name))

        id_sb = sb("id2_sb", [P, P])
        minus_half = sb("minus_half2", [P, CB])
        sc = sb("sc", [P, 4, KT])
        sc3 = sb("sc3", [P, 1])
        x_in = sb("x_in", [P, CB, D])
        x_res = sb("x_res", [P, CB, D])
        xh, xl = sb("xh", [P, CHUNK], F32R), sb("xl", [P, CHUNK], F32R)
        act_f = sb("act_f", [P, 2, CHUNK])
        gate_f = sb("gate_f", [P, 2, CHUNK])
        g1h, g1l = sb("g1h", [P, KT, CHUNK], F32R), sb("g1l", [P, KT, CHUNK], F32R)
        g2h, g2l = sb("g2h", [P, KT, CHUNK], F32R), sb("g2l", [P, KT, CHUNK], F32R)
        g3h, g3l = sb("g3h", [P, KT, CHUNK], F32R), sb("g3l", [P, KT, CHUNK], F32R)
        gelu_f = sb("gelu_f", [P, 2, CHUNK])
        y_sb = sb("y_sb", [P, CHUNK])
        res = sb("res_f", [P, CB, D])
        bn6 = sb("bn6_f", [P, CB, 6])
        meanvar = sb("meanvar_f", [P, CB, 2])
        vareps = sb("vareps_f", [P, CB])
        rstd = sb("rstd_f", [P, CB])
        y_out = sb("y_out", [P, CB, D])

        ps_r = [ctx.enter_context(nc.psum_tensor(f"ps_r{i}", [P, 512], F32)) for i in range(4)]
        ps_s = [ctx.enter_context(nc.psum_tensor(f"ps_s{i}", [P, 512], F32)) for i in range(2)]
        ps_y = ctx.enter_context(nc.psum_tensor("ps_y", [P, 512], F32))
        ps_x = ctx.enter_context(nc.psum_tensor("ps_x", [P, 512], F32))

        passed = {e: sem(f"passed2_{e}") for e in ("sp", "dve", "pool")}
        consts2 = sem("consts2")
        xin_landed, xres_landed, out_stored = sem("xin_landed"), sem("xres_landed"), sem("out_stored")
        xT_done, x_hi, x_lo = sem("x_turned"), sem("x_hi"), sem("x_lo")
        silu_in, up_in, silu_done, gate_done = sem("silu_in"), sem("up_in"), sem("silu_done"), sem("gate_done")
        g1_hi, g1_lo = sem("g1_hi"), sem("g1_lo")
        l2_done, gelu2_done, g2_lo = sem("l2_done"), sem("gelu2_done"), sem("g2_lo")
        l3_done, gelu3_done, g3_lo = sem("l3_done"), sem("gelu3_done"), sem("g3_lo")
        l4_done, y_copied, y_turned = sem("l4_done"), sem("y_copied"), sem("y_turned")
        res_done, bn_done, stats_done = sem("res2_done"), sem("bn2_done"), sem("stats2_done")
        eps_done, rstd_done, out_done = sem("eps2_done"), sem("rstd2_done"), sem("out_done")

        STEPS = dict(first=-2, loop_from=3, loop_to=CHUNKS - 3, last=CHUNKS, unroll=1)
        FIRST = STEPS["first"]

        block = ctx.enter_context(nc.Block())

        def tokens(dram, c):
            return dram[c].rearrange("a p d -> p a d")

        x1_c = x1_dram.rearrange("(c n) p a d -> c p n a d", n=CHUNK // SEQ)
        out_c = out.rearrange("(c n) (a p) d -> c p n a d", n=CHUNK // SEQ, p=P)
        NB = CHUNK // SEQ

        @block.sync
        def _(sp):
            sp.dma_start(id_sb[:], ident).then_inc(consts2, DMA)
            for i in range(4):
                sp.dma_start(sc[:, i, :], scales[i]).then_inc(consts2, DMA)
            sp.dma_start(sc3[:], scales[4]).then_inc(consts2, DMA)

            def load(dst, c, signal):
                for n in range(NB):
                    sp.dma_start(dst[:, n * BLK:(n + 1) * BLK, :], x1_c[c, :, n, :, :]).then_inc(signal, DMA)

            load(x_in, 0, xin_landed)

            def step(c, s):
                if live(c - 2, CHUNKS):
                    wait_apart(sp, out_done, c - 1, passed["sp"])
                    for n in range(NB):
                        sp.dma_start(out_c[c - 2, :, n, :, :], y_out[:, n * BLK:(n + 1) * BLK, :]).then_inc(out_stored, DMA)
                if live(c - 1, CHUNKS):
                    wait_apart(sp, res_done, c - 1, passed["sp"])
                    load(x_res, c - 1, xres_landed)
                if live(c + 3, CHUNKS):
                    wait_apart(sp, xT_done, c + 3, passed["sp"])
                    load(x_in, c + 3, xin_landed)

            drive(sp, step, **STEPS)
            sp.wait_ge(out_done, CHUNKS)
            for n in range(NB):
                sp.dma_start(out_c[CHUNKS - 1, :, n, :, :], y_out[:, n * BLK:(n + 1) * BLK, :]).then_inc(out_stored, DMA)
            sp.wait_ge(out_stored, CHUNKS * NB * DMA)

        @block.tensor
        def _(pe):
            def product(ps, o, wh, wl, ah, al, kt, ready=None):
                for k in range(kt):
                    if ready is not None:
                        ready(k)
                    w_hi, w_lo = wh[:, k, o * P:(o + 1) * P], wl[:, k, o * P:(o + 1) * P]
                    a_hi, a_lo = (ah[:, k, :], al[:, k, :]) if kt > 1 else (ah[:], al[:])
                    pe.matmul(ps[:], w_hi, a_hi, start=(k == 0), stop=False)
                    pe.matmul(ps[:], w_lo, a_hi, start=False, stop=False)
                    mm = pe.matmul(ps[:], w_hi, a_lo, start=False, stop=(k == kt - 1))
                return mm

            def step(c, s):
                if live(c, CHUNKS):
                    for o in range(KT):
                        wait(pe, gelu3_done, (c - 1) * KT + o + 1)
                        ready = (lambda k: wait(pe, g1_lo, c * KT + k + 1)) if o == 0 else None
                        product(ps_r[o], o, h1h, h1l, g1h, g1l, KT, ready).then_inc(l2_done, 1)
                if live(c - 1, CHUNKS):
                    wait(pe, res_done, c - 1)
                    product(ps_y, 0, w3h, w3l, g3h, g3l, KT,
                            lambda k: wait(pe, g3_lo, (c - 1) * KT + k + 1)).then_inc(l4_done, 1)
                if live(c + 1, CHUNKS):
                    wait(pe, x_lo, c + 2)
                    for o in range(KT):
                        wait(pe, silu_done, (c + 1) * KT + o - 1)
                        product(ps_s[o % 2], o, w1h, w1l, xh, xl, 1).then_inc(silu_in, 1)
                        if live(c, CHUNKS):
                            wait(pe, gelu2_done, c * KT + o + 1)
                        product(ps_r[o], o, w2h, w2l, xh, xl, 1).then_inc(up_in, 1)
                if live(c + 2, CHUNKS):
                    wait(pe, xin_landed, (c + 3) * NB * DMA)
                    wait(pe, x_lo, c + 2)
                    if isinstance(c, int) and c == FIRST:
                        pe.wait_ge(consts2, 6 * DMA)
                    for a in range(CB):
                        mm = pe.transpose(ps_x[:, a * P:(a + 1) * P], x_in[:, a, :], id_sb[:])
                    mm.then_inc(xT_done, 1)
                if live(c - 1, CHUNKS):
                    wait(pe, y_copied, c)
                    for a in range(CB):
                        mm = pe.transpose(ps_y[:, a * P:(a + 1) * P], y_sb[:, a * P:(a + 1) * P], id_sb[:])
                    mm.then_inc(y_turned, 1)
                if live(c, CHUNKS):
                    for o in range(KT):
                        if live(c + 1, CHUNKS):
                            wait(pe, gate_done, (c + 1) * KT + o + 1)
                        else:
                            wait(pe, gelu2_done, c * KT + o + 1)
                        ready = (lambda k: wait(pe, g2_lo, c * KT + k + 1)) if o == 0 else None
                        product(ps_r[o], o, h2h, h2l, g2h, g2l, KT, ready).then_inc(l3_done, 1)

            drive(pe, step, **STEPS)

        @block.scalar
        def _(act):
            def gelus(c, layer, in_done, out_hi, prev_use, lo_done, done):
                for o in range(KT):
                    wait(act, in_done, c * KT + o + 1)
                    wait(act, lo_done, c * KT + o - 1)
                    if o == 0 and prev_use is not None:
                        wait(act, *prev_use)
                    scale = sc[:, 2 + layer, o:o + 1]
                    nc.scalar.activation(gelu_f[:, o % 2, :], ps_r[o][:], ACT.Gelu, scale=scale)
                    nc.scalar.activation(out_hi[:, o, :], ps_r[o][:], ACT.Gelu, scale=scale).then_inc(done, 1)

            def step(c, s):
                if live(c, CHUNKS):
                    wait(act, g3_lo, c * KT)
                    gelus(c, 0, l2_done, g2h, (l3_done, c * KT), g2_lo, gelu2_done)
                if live(c - 1, CHUNKS):
                    wait(act, l4_done, c)
                    wait(act, y_turned, c - 1)
                    nc.scalar.activation(y_sb[:], ps_y[:], ACT.Copy, scale=sc3[:, 0:1]).then_inc(y_copied, 1)
                if live(c + 1, CHUNKS):
                    for o in range(KT):
                        wait(act, silu_in, (c + 1) * KT + o + 1)
                        wait(act, gate_done, (c + 1) * KT + o - 1)
                        nc.scalar.activation(act_f[:, o % 2, :], ps_s[o % 2][:], ACT.Silu,
                                             scale=sc[:, 0, o:o + 1]).then_inc(silu_done, 1)
                if live(c + 2, CHUNKS):
                    wait(act, xT_done, c + 3)
                    wait(act, up_in, (c + 2) * KT)
                    nc.scalar.activation(xh[:], ps_x[:], ACT.Copy).then_inc(x_hi, 1)
                if live(c, CHUNKS):
                    wait(act, g2_lo, (c + 1) * KT)
                    gelus(c, 1, l3_done, g3h, (l4_done, c), g3_lo, gelu3_done)

            act.wait_ge(consts2, 6 * DMA)
            drive(act, step, **STEPS)

        @block.vector
        def _(dve):
            def lows(c, hi, lo, done, signal):
                for o in range(KT):
                    wait(dve, done, c * KT + o + 1)
                    nc.vector.tensor_tensor(lo[:, o, :], gelu_f[:, o % 2, :], hi[:, o, :].bitcast(F32),
                                            ALU.subtract).then_inc(signal, 1)

            def step(c, s):
                if live(c, CHUNKS):
                    lows(c, g2h, g2l, gelu2_done, g2_lo)
                if live(c + 1, CHUNKS):
                    wait(dve, l2_done, (c + 1) * KT)
                    for o in range(KT):
                        n = (c + 1) * KT + o + 1
                        wait(dve, silu_done, n)
                        wait(dve, up_in, n)
                        nc.vector.scalar_tensor_tensor(out=gate_f[:, o % 2, :], in0=ps_r[o][:], scalar=sc[:, 1, o:o + 1],
                                                       in1=act_f[:, o % 2, :], op0=ALU.mult,
                                                       op1=ALU.mult).then_inc(gate_done, 1)
                        wait(dve, gate_done, n)
                        nc.vector.tensor_copy(g1h[:, o, :], gate_f[:, o % 2, :]).then_inc(g1_hi, 1)
                        wait(dve, g1_hi, n)
                        nc.vector.tensor_tensor(g1l[:, o, :], gate_f[:, o % 2, :], g1h[:, o, :].bitcast(F32),
                                                ALU.subtract).then_inc(g1_lo, 1)
                if live(c + 2, CHUNKS):
                    wait(dve, x_hi, c + 3)
                    nc.vector.tensor_tensor(xl[:], ps_x[:], xh[:].bitcast(F32), ALU.subtract).then_inc(x_lo, 1)
                if live(c - 1, CHUNKS):
                    wait(dve, y_turned, c)
                    wait(dve, xres_landed, c * NB * DMA)
                    wait(dve, out_done, c - 1)
                    nc.vector.tensor_tensor(res[:].rearrange("p a d -> p (a d)"), ps_y[:],
                                            x_res[:].rearrange("p a d -> p (a d)"), ALU.add).then_inc(res_done, 1)
                    wait(dve, res_done, c)
                    for a in range(CB):
                        nc.vector.bn_stats(bn6[:, a, :], res[:, a, :]).then_inc(bn_done, 1)
                    wait_apart(dve, bn_done, c * CB, passed["dve"])
                    for a in range(CB):
                        nc.vector.bn_aggr(meanvar[:, a, :], bn6[:, a, :]).then_inc(stats_done, 1)
                if live(c, CHUNKS):
                    lows(c, g3h, g3l, gelu3_done, g3_lo)

            drive(dve, step, **STEPS)

        @block.gpsimd
        def _(pool):
            nc.gpsimd.memset(minus_half[:], -0.5).then_inc(eps_done, 1)

            def step(c, s):
                if live(c - 1, CHUNKS):
                    wait_apart(pool, stats_done, c * CB, passed["pool"])
                    nc.gpsimd.tensor_scalar(vareps[:], meanvar[:, :, 1], EPS, None, ALU.add).then_inc(eps_done, 1)
                    wait(pool, eps_done, c + 1)
                    nc.gpsimd.tensor_tensor(rstd[:], vareps[:], minus_half[:], ALU.pow).then_inc(rstd_done, 1)
                    wait(pool, rstd_done, c)
                    wait_apart(pool, out_stored, (c - 1) * NB * DMA, passed["pool"])
                    for a in range(CB):
                        ins = nc.gpsimd.tensor_scalar(y_out[:, a, :], res[:, a, :], meanvar[:, a, 0:1],
                                                      rstd[:, a:a + 1], ALU.subtract, ALU.mult)
                    ins.then_inc(out_done, 1)

            drive(pool, step, **STEPS)


def build(nc, a, out):
    x1_dram = nc.dram_tensor("x1_scratch", [BATCH, P, BLK, D], F32, kind="Internal").ap()
    qk_dram = nc.dram_tensor("qk_scratch", [2, P, 4, SEQ], F32, kind="Internal").ap()
    with ExitStack() as ctx:
        wts = []
        for name, kt, n in (("w1", 1, HID), ("w2", 1, HID), ("h1", KT, HID), ("h2", KT, HID), ("w3", KT, D)):
            wts.append(tuple(ctx.enter_context(nc.sbuf_tensor(f"{name}_{part}", [P, kt, n], F32R)) for part in ("hi", "lo")))
        raw_w = [a[n].rearrange("(k p) n -> p k n", p=P) for n in ("w1T", "w2T", "h1T", "h2T", "w3T")]
        attention(nc, wts, a["x"], a["xT"], a["wqT"], a["wkT"], a["wvT"], a["woT"], a["bo"], a["qscale"], a["ident"],
                  a["tri"], a["rows"], x1_dram, qk_dram, raw_w)
        scales = [a[n] for n in ("w1_s", "w2_s", "h1_s", "h2_s", "w3_s")]
        ffn(nc, wts, scales, a["ident"], x1_dram, out)


def shape_constants():
    i = np.arange(P, dtype=np.float32)
    lower = -2.0 * np.maximum(i[:, None] - i[None, :], 0)
    pos = np.arange(SEQ, dtype=np.float32)
    sign = np.where(pos < P, 1.0, -1.0).astype(np.float32)
    rows = np.stack([sign * pos, -sign, np.ones(SEQ, np.float32), pos])
    qscale = np.repeat(1.0 / (np.array(slopes()) * np.sqrt(float(DH))), DH).astype(np.float32)
    return {
        "qscale": qscale.reshape(P, 1),
        "ident": np.eye(P, dtype=np.float32),
        "tri": np.stack([lower, lower.T]),
        "rows": np.ascontiguousarray(np.tile(rows, (1, HEADS))),
    }


def kernel(**inputs):
    import concourse.bacc as bacc
    from concourse.bass_utils import run_bass_kernel_spmd

    x = inputs["L0_attn_x"]
    laid = {
        "x": x, "xT": x.transpose(0, 2, 1),
        "wqT": inputs["L0_attn_wq"].T, "wkT": inputs["L0_attn_wk"].T, "wvT": inputs["L0_attn_wv"].T,
        "woT": inputs["L0_attn_wo"].T, "bo": np.broadcast_to(inputs["L0_attn_bo"], (P, D)),
        "w1T": inputs["L0_ffn_w1_w"].T, "w2T": inputs["L0_ffn_w2_w"].T, "h1T": inputs["L0_ffn_h1_w"].T,
        "h2T": inputs["L0_ffn_h2_w"].T, "w3T": inputs["L0_ffn_w3_w"].T,
        **{f"{n}_s": inputs[f"L0_ffn_{n}_s"].reshape(-1, P).T for n in ("w1", "w2", "h1", "h2", "w3")},
        **shape_constants(),
    }
    nc = bacc.Bacc("TRN2", target_bir_lowering=False, num_devices=1)
    arrays, operands = {}, {}
    for name, value in laid.items():
        value = np.ascontiguousarray(value)
        arrays[f"in_{name}"] = value
        operands[name] = nc.dram_tensor(f"in_{name}", value.shape, mybir.dt.from_np(value.dtype), kind="ExternalInput").ap()
    out = nc.dram_tensor("out_0", (BATCH, SEQ, D), F32, kind="ExternalOutput").ap()
    build(nc, operands, out)
    r = run_bass_kernel_spmd(nc, [arrays], core_ids=[0])
    return r.results[0]["out_0"]
```

```python
from contextlib import ExitStack

import numpy as np

import concourse.bass as bass
from concourse import mybir

F32 = mybir.dt.float32
F32R = mybir.dt.float32r
BF16 = mybir.dt.bfloat16
ACT = mybir.ActivationFunctionType
ALU = mybir.AluOpType
AX_X = mybir.AxisListType.X
AX_XY = mybir.AxisListType.XY

P = 128
BATCH = 32
SEQ = 256
D = 128
HEADS = 16
DH = D // HEADS
BLK = SEQ // P
HALF = HEADS // 2
GROUP = 4
VCOLS = 32
HID = 512
KT = HID // P
CHUNK = 512
CB = CHUNK // P
CHUNKS = BATCH * SEQ // CHUNK
EPS = 1e-5
RAW_BUFS = 4
N_PIECES = 11
DMA = 16

STACK = 3 * DH
MROW = P - 2
KA = MROW
STEPS_T = (MROW - STACK - 4) // BLK
CORNER = P - STEPS_T
QH, QL, KH, KL = range(4)


def slopes():
    start = 2.0 ** (-2.0 ** (-(np.log2(HEADS) - 3)))
    return [float(np.float32(start * start ** i)) for i in range(HEADS)]


def runs(n_or_value):
    return not isinstance(n_or_value, int) or n_or_value > 0


def wait(eng, sem, value):
    if runs(value):
        eng.wait_ge(sem, value)


def wait_apart(eng, sem, value, passed):
    wait(eng, sem, value)
    if not isinstance(value, int):
        eng.sem_inc(passed, 1)


A_BANK = [1 if h == 3 else (h - 4) % HEADS % 3 for h in range(HEADS)]


def a_released(b, h):
    before = [g for g in range(h - HEADS, h) if A_BANK[g % HEADS] == A_BANK[h]][-1]
    return b * HEADS + before + 1


def live(index, count):
    return not isinstance(index, int) or 0 <= index < count


def drive(eng, step, first, loop_from, loop_to, last, unroll):
    for t in range(first, loop_from):
        step(t, t % 2)
    with eng.Fori(0, (loop_to - loop_from) // unroll, 1) as i:
        for u in range(unroll):
            step(i * unroll + (loop_from + u), (loop_from + u) % 2)
    for t in range(loop_to, last + 1):
        step(t, t % 2)


def attention(nc, wts, x, xT, wqT, wkT, wvT, woT, bo, qscale, ident, corner, rows, x1_dram, qk_dram, raw_w, lo_max):
    slope = slopes()
    with ExitStack() as ctx:
        def sb(name, shape, dt=F32):
            return ctx.enter_context(nc.sbuf_tensor(name, shape, dt))

        def sem(name):
            return ctx.enter_context(nc.semaphore(name))

        wq_sb, wk_sb, wv_sb, wo_sb = (sb(n, [P, D]) for n in ("wq_sb", "wk_sb", "wv_sb", "wo_sb"))
        bo_sb = sb("bo_sb", [P, D])
        qscale_sb = sb("qscale_sb", [P, 1])
        id_sb = sb("id_sb", [P, P])
        idb_sb = sb("idb_sb", [P, P], BF16)
        corner_f = sb("corner_f", [P, CORNER])
        corner_sb = sb("corner_sb", [P, BLK, CORNER], BF16)
        rows_sb = sb("rows_sb", [P, 2, SEQ])
        minus_half = sb("minus_half", [P, BLK])
        qk_stack = [sb(f"qk_stack{i}", [P, 2, HEADS, SEQ], F32R) for i in range(2)]
        q_stack, k_stack = ([tile[:, n, :, :] for tile in qk_stack] for n in range(2))
        probs = sb("probs", [P, HALF, BLK * SEQ])
        v_aug = [sb(f"v_aug{i}", [P, BLK, HEADS, VCOLS]) for i in range(2)]
        xT_sb = [sb(f"xT_sb{i}", [P, SEQ]) for i in range(2)]
        qk_sb = sb("qk_sb", [P, 4, SEQ], F32R)
        x_sb = [sb(f"x_sb{i}", [P, BLK, D]) for i in range(2)]
        xb_sb = [sb(f"xb_sb{i}", [P, BLK, D]) for i in range(2)]
        corner_rows = sb("corner_rows", [P, BLK, SEQ])
        scored = sb("scored", [P, 2, BLK, SEQ])
        negmax = sb("negmax", [P, 2, HALF, BLK])
        mrow_hi = [sb(f"mrow_hi{i}", [BLK * HALF, P], F32R) for i in range(2)]
        mrow_lo = [sb(f"mrow_lo{i}", [BLK * HALF, P], F32R) for i in range(2)]
        o_sb = sb("o_sb", [P, HEADS // GROUP, SEQ])
        recip = sb("recip", [P, BLK, HEADS])
        o_norm = sb("o_norm", [P, BLK, D])
        oT_sb = sb("oT_sb", [P, SEQ])
        res = [sb(f"res{i}", [P, BLK, D]) for i in range(2)]
        bn6 = sb("bn6", [P, BLK, 6])
        meanvar = [sb(f"meanvar{i}", [P, BLK, 2]) for i in range(2)]
        vareps = sb("vareps", [P, BLK])
        rstd = sb("rstd", [P, BLK])
        x1_sb = [sb(f"x1_sb{i}", [P, BLK, D]) for i in range(2)]
        raw = sb("raw", [P, RAW_BUFS, HID])

        ps_a = [ctx.enter_context(nc.psum_tensor(f"ps_a{i}", [P, 512], F32)) for i in range(3)]
        ps_b = [ctx.enter_context(nc.psum_tensor(f"ps_b{i}", [P, 512], F32)) for i in range(2)]
        ps_o = ctx.enter_context(nc.psum_tensor("ps_o", [P, 2, SEQ], F32))
        ps_m = [ctx.enter_context(nc.psum_tensor(f"ps_m{i}", [P, 512], F32)) for i in range(2)]

        passed = {e: sem(f"passed_{e}") for e in ("sp", "dve", "pool")}
        qk_const_landed = sem("qk_const_landed")
        const_landed = sem("const_landed")
        const_set = sem("const_set")
        rows_landed = sem("rows_landed")
        rows_laid = [sem(f"rows_laid{i}") for i in range(2)]
        v_laid = sem("v_laid")
        xT_landed, x_landed = sem("xT_landed"), sem("x_landed")
        qk_done, qk_hi, qk_lo = sem("qk_done"), sem("qk_hi"), sem("qk_lo")
        spilled = sem("spilled")
        corner_zero, corner_laid = sem("corner_zero"), sem("corner_laid")
        stacked = [sem(f"stacked{i}") for i in range(2)]
        v_done, v_copied = sem("v_done"), sem("v_copied")
        scores_a, max_done = sem("scores_a"), sem("max_done")
        mT_done, m_hi, m_lo = sem("mT_done"), sem("m_hi"), sem("m_lo")
        m_landed = [sem(f"m_landed{i}") for i in range(2)]
        scores_b, exp_done = sem("scores_b"), sem("exp_done")
        pv_done, o_copied = sem("pv_done"), sem("o_copied")
        o_turned, recip_done, normed = sem("o_turned"), sem("recip_done"), sem("normed")
        oT_done, oT_copied = sem("oT_done"), sem("oT_copied")
        wo_done, res_done = sem("wo_done"), sem("res_done")
        bn_done, stats_done = sem("bn_done"), sem("stats_done")
        eps_done, rstd_done = sem("eps_done"), sem("rstd_done")
        xb_done, x1_done, x1_stored = sem("xb_done"), sem("x1_done"), sem("x1_stored")
        raw_landed, raw_split = [sem(f"raw_landed{i}") for i in range(RAW_BUFS)], sem("raw_split")
        raw_hi, lo_seen = sem("raw_hi"), sem("lo_seen")

        pieces = []
        for (hi, lo), src in zip(wts, raw_w):
            kt, n = src.shape[1:]
            for a in range(0, kt, HID // n):
                pieces.append(tuple(w[:, a:a + HID // n, :] for w in (hi, lo, src)))
        piece_at = [(-2, 8)] * RAW_BUFS + [(0, 11), (1, 11), (2, 11), (BATCH - 3, 11), (BATCH - 2, 11),
                                           (BATCH - 1, 4), (BATCH - 1, 10)]
        assert len(pieces) == N_PIECES == len(piece_at)

        def pieces_of(t, k):
            return [n for n, (step, head) in enumerate(piece_at) if step == t and k in (None, head)]

        def raw_piece(n):
            width = pieces[n][2].shape[2]
            return raw[:, n % RAW_BUFS, :].rearrange("p (k n) -> p k n", n=width)
        N_CONST, N_QK_CONST = 5, 3
        STEPS = dict(first=-2, loop_from=3, loop_to=BATCH - 3, last=BATCH, unroll=2)
        FIRST = STEPS["first"]

        block = ctx.enter_context(nc.Block())

        @block.sync
        def _(sp):
            sp.dma_start(xT_sb[0][:], xT[0]).then_inc(xT_landed, DMA)
            sp.dma_start(rows_sb[:], rows).then_inc(rows_landed, DMA)
            for dst, src in ((wq_sb, wqT), (wk_sb, wkT), (qscale_sb, qscale)):
                sp.dma_start(dst[:], src).then_inc(qk_const_landed, DMA)
            for dst, src in ((id_sb, ident), (corner_f, corner), (wv_sb, wvT), (wo_sb, woT), (bo_sb, bo)):
                sp.dma_start(dst[:], src).then_inc(const_landed, DMA)
            sp.wait_ge(xT_landed, DMA)
            sp.dma_start(xT_sb[1][:], xT[1]).then_inc(xT_landed, DMA)
            sp.dma_start(x_sb[0][:], x[0].rearrange("(a p) d -> p a d", p=P)).then_inc(x_landed, DMA)

            def stack(b, par, hf):
                heads = slice(hf * HALF, (hf + 1) * HALF)
                sp.dma_start(qk_stack[par][0:STACK, :, heads, :].bitcast(F32),
                             qk_dram[par, :, :, :, heads, :].rearrange("n r d h t -> (r d) n h t")).then_inc(stacked[hf], DMA)

            def spill(par):
                src = qk_sb[:].bitcast(F32)
                flat = qk_dram[par].rearrange("n r d h t -> (d h) (n r) t")
                sp.dma_start(flat[:, 1:5, :], src).then_inc(spilled, DMA)
                sp.dma_start(flat[:, 0:6:5, :], src[:, QH:KL:KH, :]).then_inc(spilled, DMA)

            def max_rows(b, par, hf):
                wait_apart(sp, m_lo, b * 2 + hf + 1, passed["sp"])
                for r, src in enumerate((mrow_hi[hf], mrow_lo[hf])):
                    dst = q_stack[par][MROW + r:MROW + r + 1, hf * HALF:(hf + 1) * HALF, :]
                    sp.dma_start(dst.bitcast(F32).rearrange("p h (b q) -> p (h b) q", b=BLK),
                                 src[:].bitcast(F32)).then_inc(m_landed[hf], DMA)

            def step(t, s):
                if live(t + 1, BATCH):
                    wait_apart(sp, spilled, (t + 2) * 2 * DMA, passed["sp"])
                    wait_apart(sp, scores_b, t * HEADS, passed["sp"])
                    stack(t + 1, 1 - s, 1)
                if live(t, BATCH):
                    max_rows(t, s, 1)
                if live(t - 2, BATCH):
                    wait_apart(sp, x1_done, t - 1, passed["sp"])
                    wait_apart(sp, x1_stored, (t - 2) * DMA, passed["sp"])
                    sp.dma_start(x1_dram[t - 2], x1_sb[s][:]).then_inc(x1_stored, DMA)
                if live(t + 3, BATCH) and live(t + 1, BATCH):
                    wait_apart(sp, v_done, t + 2, passed["sp"])
                    wait_apart(sp, xT_landed, (t + 3) * DMA, passed["sp"])
                    sp.dma_start(xT_sb[1 - s][:], xT[t + 3]).then_inc(xT_landed, DMA)
                if live(t + 2, BATCH):
                    wait_apart(sp, qk_lo, (t + 2) * 2 + 2, passed["sp"])
                    if live(t, BATCH):
                        wait_apart(sp, stacked[0], (t + 1) * DMA, passed["sp"])
                        wait_apart(sp, stacked[1], (t + 1) * DMA, passed["sp"])
                    spill(s)
                    wait_apart(sp, spilled, (t + 3) * 2 * DMA, passed["sp"])
                    if live(t, BATCH):
                        wait_apart(sp, scores_b, t * HEADS + HALF, passed["sp"])
                    if isinstance(t, int) and t < 0:
                        sp.wait_ge(rows_laid[s], 3)
                    stack(t + 2, s, 0)
                if live(t + 1, BATCH):
                    max_rows(t + 1, 1 - s, 0)
                if live(t + 1, BATCH) and live(t, BATCH):
                    wait_apart(sp, xb_done, t, passed["sp"])
                    wait_apart(sp, x_landed, (t + 1) * DMA, passed["sp"])
                    sp.dma_start(x_sb[1 - s][:], x[t + 1].rearrange("(a p) d -> p a d", p=P)).then_inc(x_landed, DMA)

            drive(sp, step, **STEPS)
            sp.wait_ge(x1_done, BATCH)
            sp.wait_ge(x1_stored, (BATCH - 1) * DMA)
            sp.dma_start(x1_dram[BATCH - 1], x1_sb[(BATCH - 1) % 2][:]).then_inc(x1_stored, DMA)
            sp.wait_ge(x1_stored, BATCH * DMA)

        @block.tensor
        def _(pe):
            def add_corner(ps):
                out = ps[:].rearrange("p (b c) -> p b c", c=P)[:, 0:4:3, STEPS_T:P]
                return pe.matmul(out, idb_sb[:], corner_sb[:], start=False, stop=True, skip_group_check=True)

            def score_max(b, par, h):
                if h % HALF == 0:
                    wait(pe, stacked[h // HALF], (b + 1) * DMA)
                wait(pe, max_done, a_released(b, h))
                ps = ps_a[A_BANK[h]]
                for qb in range(BLK):
                    mm = pe.matmul(ps[:, qb * SEQ:(qb + 1) * SEQ], q_stack[par][0:KA, h, qb * P:(qb + 1) * P],
                              k_stack[par][0:KA, h, :], start=(qb == 0), stop=True,
                              skip_group_check=True)
                mm.then_inc(scores_a, 1)

            def score_exp(b, par, h):
                if h % HALF == 0:
                    wait(pe, m_landed[h // HALF], (b + 1) * 2 * DMA)
                wait(pe, exp_done, b * HEADS + h - 1)
                ps = ps_b[h % 2]
                for kb in range(BLK):
                    pe.matmul(ps[:, kb * SEQ:(kb + 1) * SEQ], k_stack[par][:, h, kb * P:(kb + 1) * P],
                              q_stack[par][:, h, :], start=(kb == 0), stop=False, skip_group_check=True)

            def pv(b, par, j):
                if j == 0:
                    wait(pe, v_copied, b + 1)
                wait(pe, exp_done, b * HEADS + GROUP * (j + 1))
                if j % 2 == 0:
                    wait(pe, o_copied, b * 2 + j // 2)
                for kb in range(BLK):
                    for g in range(GROUP):
                        h = j * GROUP + g
                        mm = pe.matmul(ps_o[VCOLS * g:VCOLS * (g + 1), j % 2, :],
                                       v_aug[par][:, kb, h, :], probs[:, h % HALF, kb * SEQ:(kb + 1) * SEQ],
                                       start=(kb == 0), stop=(kb == BLK - 1), skip_group_check=True)
                mm.then_inc(pv_done, 1)

            def turn_max(b, hf):
                wait(pe, max_done, b * HEADS + (hf + 1) * HALF)
                pe.transpose(ps_m[0][0:BLK * HALF, 0:P], negmax[:, hf, :, :].rearrange("p h a -> p (h a)"),
                             id_sb[:]).then_inc(mT_done, 1)

            def turn_o(b, qb):
                wait(pe, o_copied, b * 2 + 2)
                for j in range(HEADS // GROUP):
                    mm = pe.transpose(ps_m[qb][:, j * P:(j + 1) * P], o_sb[:, j, qb * P:(qb + 1) * P], id_sb[:])
                mm.then_inc(o_turned, 1)

            def step(t, s):
                if isinstance(t, int) and t == FIRST + 1:
                    pe.wait_ge(const_landed, N_CONST * DMA)
                    pe.wait_ge(const_set, 2)
                for k in range(HEADS):
                    if live(t + 1, BATCH):
                        score_max(t + 1, 1 - s, k)
                    if live(t, BATCH):
                        score_exp(t, s, k)
                    if live(t, BATCH):
                        add_corner(ps_b[k % 2]).then_inc(scores_b, 1)
                        if k >= 5 and k % GROUP == 1:
                            pv(t, s, k // GROUP - 1)
                    if k == 1 and live(t - 1, BATCH):
                        pv(t - 1, 1 - s, 3)
                    if k == 1 and live(t, BATCH):
                        wait(pe, m_lo, t * 2 + 1)
                        turn_max(t, 1)
                    if k == 2 and live(t + 1, BATCH):
                        wait(pe, xT_landed, (t + 2) * DMA)
                        if live(t - 2, BATCH):
                            wait(pe, res_done, t - 1)
                        elif live(t, BATCH):
                            wait(pe, v_copied, t + 1)
                        for tb in range(BLK):
                            mm = pe.matmul(ps_m[1][:, tb * D:(tb + 1) * D], xT_sb[1 - s][:, tb * P:(tb + 1) * P], wv_sb[:],
                                           start=True, stop=True)
                        mm.then_inc(v_done, 1)
                    if k == 3 and live(t + 2, BATCH):
                        wait(pe, xT_landed, (t + 3) * DMA)
                        if live(t, BATCH):
                            wait(pe, m_lo, t * 2 + 2)
                        else:
                            wait(pe, qk_lo, (t + 1) * 2 + 2)
                        if isinstance(t, int) and t == FIRST:
                            pe.wait_ge(qk_const_landed, N_QK_CONST * DMA)
                        for n, w in enumerate((wq_sb, wk_sb)):
                            mm = pe.matmul(ps_m[0][:, n * SEQ:(n + 1) * SEQ], w[:], xT_sb[s][:], start=True, stop=True)
                        mm.then_inc(qk_done, 1)
                    if k == 6 and live(t - 1, BATCH):
                        if live(t + 2, BATCH):
                            wait(pe, qk_lo, (t + 2) * 2 + 2)
                        elif live(t, BATCH):
                            wait(pe, m_lo, t * 2 + 2)
                        else:
                            wait(pe, normed, (t - 2) * 2 + 1)
                        turn_o(t - 1, 0)
                    if k == 7 and live(t - 1, BATCH):
                        if live(t + 1, BATCH):
                            wait(pe, v_copied, t + 2)
                        else:
                            wait(pe, res_done, t - 1)
                        turn_o(t - 1, 1)
                    if k == 10 and live(t - 1, BATCH):
                        wait(pe, normed, (t - 1) * 2 + 2)
                        for qb in range(BLK):
                            mm = pe.transpose(ps_m[1][:, qb * P:(qb + 1) * P], o_norm[:, qb, :], id_sb[:])
                        mm.then_inc(oT_done, 1)
                    if k == 9 and live(t + 1, BATCH):
                        if live(t - 1, BATCH):
                            wait(pe, normed, (t - 1) * 2 + 1)
                        else:
                            wait(pe, qk_lo, (t + 2) * 2 + 2)
                        turn_max(t + 1, 0)
                    if k == 12 and live(t - 1, BATCH):
                        wait(pe, oT_copied, t)
                        for qb in range(BLK):
                            mm = pe.matmul(ps_m[1][:, qb * D:(qb + 1) * D], oT_sb[:, qb * P:(qb + 1) * P], wo_sb[:],
                                           start=True, stop=True)
                        mm.then_inc(wo_done, 1)

            drive(pe, step, **STEPS)

        @block.scalar
        def _(act):
            def max_hi(b, hf):
                wait(act, mT_done, b * 2 + hf + 1)
                wait(act, m_landed[hf], b * 2 * DMA)
                nc.scalar.activation(mrow_hi[hf][:], ps_m[0][0:BLK * HALF, 0:P], ACT.Copy).then_inc(m_hi, 1)

            def copy_o(b, hf):
                wait(act, pv_done, b * 4 + hf * 2 + 2)
                wait(act, o_turned, b * 2)
                nc.scalar.activation(o_sb[:, 2 * hf:2 * hf + 2, :], ps_o[:], ACT.Copy).then_inc(o_copied, 1)

            def lay_rows(i, first, last):
                nc.scalar.activation(qk_stack[i][:, 1, first:last, :],
                                     rows_sb[:, 1, :].unsqueeze(1).broadcast_to([P, last - first, SEQ]),
                                     ACT.Copy).then_inc(rows_laid[i], 1)

            def step(t, s):
                for k in range(HEADS):
                    if live(t, BATCH):
                        wait(act, scores_b, t * HEADS + k + 1)
                        if k % GROUP == 0:
                            wait(act, pv_done, t * 4 + k // GROUP - 1)
                        nc.scalar.activation(probs[:, k % HALF, :], ps_b[k % 2][:], ACT.Exp,
                                             scale=slope[k]).then_inc(exp_done, 1)
                    if k == 1 and live(t, BATCH):
                        max_hi(t, 1)
                    if k == 2 and live(t - 1, BATCH):
                        copy_o(t - 1, 1)
                    if k == 3 and live(t + 1, BATCH):
                        wait(act, v_done, t + 2)
                        wait(act, pv_done, t * 4)
                        if isinstance(t, int) and t < 1:
                            act.wait_ge(v_laid, 4)
                        nc.scalar.activation(v_aug[1 - s][:, :, :, 0:DH],
                                             ps_m[1][:, 0:BLK * D].rearrange("p (a h d) -> p a h d", a=BLK, d=DH),
                                             ACT.Copy).then_inc(v_copied, 1)
                    if k == 4 and live(t + 2, BATCH):
                        wait(act, qk_done, t + 3)
                        wait(act, spilled, (t + 2) * 2 * DMA)
                        nc.scalar.activation(qk_sb[:, QH, :], ps_m[0][:, 0:SEQ], ACT.Copy,
                                             scale=qscale_sb[:, 0:1]).then_inc(qk_hi, 1)
                        nc.scalar.activation(qk_sb[:, KH, :], ps_m[0][:, SEQ:2 * SEQ], ACT.Copy).then_inc(qk_hi, 1)
                    if k == 10 and live(t + 1, BATCH):
                        max_hi(t + 1, 0)
                    if k == 10 and live(t - 1, BATCH):
                        wait(act, oT_done, t)
                        wait(act, wo_done, t - 1)
                        nc.scalar.activation(oT_sb[:], ps_m[1][:, 0:SEQ], ACT.Copy).then_inc(oT_copied, 1)
                    if k == 10 and live(t, BATCH):
                        copy_o(t, 0)
                    if isinstance(t, int):
                        for n in pieces_of(t, k):
                            act.wait_ge(raw_landed[n % RAW_BUFS], (n // RAW_BUFS + 1) * DMA)
                            nc.scalar.activation(pieces[n][0], raw_piece(n), ACT.Copy).then_inc(raw_hi, 1)
                    if isinstance(t, int) and t == FIRST and k == 5:
                        lay_rows(0, HALF, HEADS)
                    if isinstance(t, int) and t == FIRST and k == 15:
                        lay_rows(1, 0, HALF)
                        lay_rows(1, HALF, HEADS)

            act.wait_ge(rows_landed, DMA)
            lay_rows(0, 0, HALF)
            act.wait_ge(qk_const_landed, N_QK_CONST * DMA)
            drive(act, step, **STEPS)

        @block.vector
        def _(dve):
            def lay_rows(i):
                nc.vector.tensor_copy(qk_stack[i][:, 0, :, :], rows_sb[:, 0, :].unsqueeze(1).broadcast_to([P, HEADS, SEQ])
                                      ).then_inc(rows_laid[i], 1)

            def lay_constants():
                dve.wait_ge(const_landed, N_CONST * DMA)
                dve.wait_ge(corner_zero, 1)
                nc.vector.tensor_copy(idb_sb[:], id_sb[:]).then_inc(const_set, 1)
                nc.vector.tensor_copy(corner_sb[:], corner_f[:].unsqueeze(1).broadcast_to([P, BLK, CORNER])).then_inc(const_set, 1)
                for qb in range(BLK):
                    nc.vector.tensor_copy(corner_rows[:, qb, qb * P + STEPS_T:(qb + 1) * P], corner_f[:]).then_inc(corner_laid, 1)
                dve.wait_ge(corner_laid, 2)

            def max_lo(b, hf):
                wait(dve, m_hi, b * 2 + hf + 1)
                nc.vector.tensor_tensor(mrow_lo[hf][:], ps_m[0][0:BLK * HALF, 0:P], mrow_hi[hf][:].bitcast(F32),
                                        ALU.subtract).then_inc(m_lo, 1)

            def normalise(b, qb):
                quad = ps_m[qb][:].rearrange("p (h c) -> p h c", c=VCOLS)
                wait(dve, o_turned, b * 2 + qb + 1)
                nc.vector.reciprocal(recip[:, qb, :], quad[:, :, DH]).then_inc(recip_done, 1)
                wait(dve, oT_done, b)
                wait(dve, recip_done, b * 2 + qb + 1)
                nc.vector.tensor_tensor(o_norm[:, qb, :].rearrange("p (h d) -> p h d", d=DH), quad[:, :, 0:DH],
                                        recip[:, qb, :].unsqueeze(2).broadcast_to([P, HEADS, DH]),
                                        ALU.mult).then_inc(normed, 1)

            def step(t, s):
                for k in range(HEADS):
                    if live(t + 1, BATCH):
                        if k % HALF == 0:
                            wait(dve, mT_done, (t + 1) * 2 + k // HALF - 1)
                        wait(dve, max_done, (t + 1) * HEADS + k - 1)
                        wait_apart(dve, scores_a, (t + 1) * HEADS + k + 1, passed["dve"])
                        for qb in range(BLK):
                            ins = nc.vector.tensor_tensor_reduce(
                                scored[:, k % 2, qb, :], ps_a[A_BANK[k]][:, qb * SEQ:(qb + 1) * SEQ], corner_rows[:, qb, :], -1.0, 3e38,
                                ALU.add, ALU.min, negmax[:, k // HALF, k % HALF, qb:qb + 1])
                        ins.then_inc(max_done, 1)
                    if k == 2 and live(t, BATCH):
                        max_lo(t, 1)
                    if k == 5 and live(t + 2, BATCH):
                        wait(dve, qk_hi, (t + 3) * 2)
                        nc.vector.scalar_tensor_tensor(
                            out=qk_sb[:, QL, :], in0=ps_m[0][:, 0:SEQ], scalar=qscale_sb[:, 0:1],
                            in1=qk_sb[:, QH, :].bitcast(F32), op0=ALU.mult, op1=ALU.subtract).then_inc(qk_lo, 1)
                        nc.vector.tensor_tensor(qk_sb[:, KL, :], ps_m[0][:, SEQ:2 * SEQ], qk_sb[:, KH, :].bitcast(F32),
                                                ALU.subtract).then_inc(qk_lo, 1)
                    if k in (7, 8) and live(t - 1, BATCH):
                        normalise(t - 1, k - 7)
                    if k == 10 and live(t + 1, BATCH):
                        max_lo(t + 1, 0)
                    if k == 13 and live(t - 1, BATCH):
                        wait(dve, wo_done, t)
                        wait(dve, xb_done, t)
                        wait(dve, x1_done, t - 2)
                        r = res[1 - s]
                        nc.vector.tensor_tensor(r[:].rearrange("p a d -> p (a d)"), ps_m[1][:, 0:BLK * D],
                                                xb_sb[1 - s][:].rearrange("p a d -> p (a d)"), ALU.add).then_inc(res_done, 1)
                        wait(dve, res_done, t)
                        for a in range(BLK):
                            nc.vector.bn_stats(bn6[:, a, :], res[1 - s][:, a, :]).then_inc(bn_done, 1)
                    if k == 14 and live(t - 1, BATCH):
                        wait_apart(dve, bn_done, t * BLK, passed["dve"])
                        for a in range(BLK):
                            nc.vector.bn_aggr(meanvar[1 - s][:, a, :], bn6[:, a, :]).then_inc(stats_done, 1)
                    if isinstance(t, int):
                        for n in pieces_of(t, k - 1):
                            hi, lo, _ = pieces[n]
                            dve.wait_ge(raw_hi, n + 1)
                            nc.vector.tensor_tensor(lo, raw_piece(n), hi.bitcast(F32), ALU.subtract).then_inc(raw_split, 1)
                        for n in pieces_of(t, k - 3):
                            dve.wait_ge(raw_split, n + 1)
                            nc.vector.tensor_reduce(lo_max[:, n:n + 1], pieces[n][1].bitcast(F32), AX_XY, ALU.max,
                                                    apply_absolute_value=True).then_inc(lo_seen, 1)
                    if isinstance(t, int) and t == FIRST and k == 6:
                        lay_constants()
                    if isinstance(t, int) and t == FIRST and k == 15:
                        lay_rows(1)

            nc.vector.memset(corner_rows[:], 0.0).then_inc(corner_zero, 1)
            dve.wait_ge(rows_landed, DMA)
            lay_rows(0)
            drive(dve, step, **STEPS)

        @block.gpsimd
        def _(pool):
            for i in range(2):
                nc.gpsimd.memset(v_aug[i][:, :, :, DH + 1:VCOLS], 0.0).then_inc(v_laid, 1)
                nc.gpsimd.memset(v_aug[i][:, :, :, DH:DH + 1], 1.0).then_inc(v_laid, 1)
            nc.gpsimd.memset(minus_half[:], -0.5).then_inc(eps_done, 1)
            bo_b = bo_sb[:].unsqueeze(1).broadcast_to([P, BLK, D])

            def step(t, s):
                if isinstance(t, int):
                    for n in pieces_of(t, None):
                        if n >= RAW_BUFS:
                            pool.wait_ge(raw_split, n - RAW_BUFS + 1)
                        nc.gpsimd.dma_start(raw_piece(n), pieces[n][2]).then_inc(raw_landed[n % RAW_BUFS], DMA)
                if live(t, BATCH):
                    if isinstance(t, int) and t == 0:
                        pool.wait_ge(const_landed, N_CONST * DMA)
                    wait(pool, x_landed, (t + 1) * DMA)
                    wait(pool, res_done, t - 1)
                    nc.gpsimd.tensor_tensor(xb_sb[s][:], x_sb[s][:], bo_b, ALU.add).then_inc(xb_done, 1)
                if live(t - 1, BATCH):
                    mv = meanvar[1 - s]
                    wait_apart(pool, stats_done, t * BLK, passed["pool"])
                    nc.gpsimd.tensor_scalar(vareps[:], mv[:, :, 1], EPS, None, ALU.add).then_inc(eps_done, 1)
                    wait(pool, eps_done, t + 1)
                    nc.gpsimd.tensor_tensor(rstd[:], vareps[:], minus_half[:], ALU.pow).then_inc(rstd_done, 1)
                    wait(pool, rstd_done, t)
                    wait_apart(pool, x1_stored, (t - 2) * DMA, passed["pool"])
                    for a in range(BLK):
                        ins = nc.gpsimd.tensor_scalar(x1_sb[1 - s][:, a, :], res[1 - s][:, a, :], mv[:, a, 0:1],
                                                      rstd[:, a:a + 1], ALU.subtract, ALU.mult)
                    ins.then_inc(x1_done, 1)

            drive(pool, step, **STEPS)


def ffn(nc, wts, scales, ident, x1_dram, out, lo_max):
    (w1h, w1l), (w2h, w2l), (h1h, h1l), (h2h, h2l), (w3h, w3l) = wts
    with ExitStack() as ctx:
        def sb(name, shape, dt=F32):
            return ctx.enter_context(nc.sbuf_tensor(name, shape, dt))

        def sem(name):
            return ctx.enter_context(nc.semaphore(name))

        id_sb = sb("id2_sb", [P, P])
        minus_half = sb("minus_half2", [P, CB])
        sc = sb("sc", [P, 4, KT])
        sc3 = sb("sc3", [P, 1])
        x_in = sb("x_in", [P, CB, D])
        x_res = sb("x_res", [P, CB, D])
        xh, xl = sb("xh", [P, CHUNK], F32R), sb("xl", [P, CHUNK], F32R)
        act_f = sb("act_f", [P, 2, CHUNK])
        gate_f = sb("gate_f", [P, 2, CHUNK])
        g1h, g1l = sb("g1h", [P, KT, CHUNK], F32R), sb("g1l", [P, KT, CHUNK], F32R)
        g2h, g2l = sb("g2h", [P, KT, CHUNK], F32R), sb("g2l", [P, KT, CHUNK], F32R)
        g3h, g3l = sb("g3h", [P, KT, CHUNK], F32R), sb("g3l", [P, KT, CHUNK], F32R)
        gelu_f = sb("gelu_f", [P, 2, CHUNK])
        y_sb = sb("y_sb", [P, CHUNK])
        res = sb("res_f", [P, CB, D])
        bn6 = sb("bn6_f", [P, CB, 6])
        meanvar = sb("meanvar_f", [P, CB, 2])
        vareps = sb("vareps_f", [P, CB])
        rstd = sb("rstd_f", [P, CB])
        y_out = sb("y_out", [P, CB, D])
        ones = sb("ones", [P, P])
        has_lo = sb("has_lo", [P, N_PIECES])
        flag = sb("flag", [1, 1])

        ps_r = [ctx.enter_context(nc.psum_tensor(f"ps_r{i}", [P, 512], F32)) for i in range(4)]
        ps_s = [ctx.enter_context(nc.psum_tensor(f"ps_s{i}", [P, 512], F32)) for i in range(2)]
        ps_y = ctx.enter_context(nc.psum_tensor("ps_y", [P, 512], F32))
        ps_x = ctx.enter_context(nc.psum_tensor("ps_x", [P, 512], F32))

        passed = {e: sem(f"passed2_{e}") for e in ("sp", "dve", "pool")}
        consts2 = sem("consts2")
        xin_landed, xres_landed, out_stored = sem("xin_landed"), sem("xres_landed"), sem("out_stored")
        xT_done, x_hi, x_lo = sem("x_turned"), sem("x_hi"), sem("x_lo")
        silu_in, up_in, silu_done, gate_done = sem("silu_in"), sem("up_in"), sem("silu_done"), sem("gate_done")
        g1_hi, g1_lo = sem("g1_hi"), sem("g1_lo")
        l2_done, gelu2_done, g2_lo = sem("l2_done"), sem("gelu2_done"), sem("g2_lo")
        l3_done, gelu3_done, g3_lo = sem("l3_done"), sem("gelu3_done"), sem("g3_lo")
        l4_done, y_copied, y_turned = sem("l4_done"), sem("y_copied"), sem("y_turned")
        res_done, bn_done, stats_done = sem("res2_done"), sem("bn2_done"), sem("stats2_done")
        eps_done, rstd_done, out_done = sem("eps2_done"), sem("rstd2_done"), sem("out_done")
        ones_set, lo_marked, lo_counted, flag_set = sem("ones_set"), sem("lo_marked"), sem("lo_counted"), sem("flag_set")

        STEPS = dict(first=-2, loop_from=3, loop_to=CHUNKS - 3, last=CHUNKS, unroll=1)
        FIRST = STEPS["first"]

        block = ctx.enter_context(nc.Block())

        def tokens(dram, c):
            return dram[c].rearrange("a p d -> p a d")

        x1_c = x1_dram.rearrange("(c n) p a d -> c p n a d", n=CHUNK // SEQ)
        out_c = out.rearrange("(c n) (a p) d -> c p n a d", n=CHUNK // SEQ, p=P)
        NB = CHUNK // SEQ

        @block.sync
        def _(sp):
            sp.dma_start(id_sb[:], ident).then_inc(consts2, DMA)
            for i in range(4):
                sp.dma_start(sc[:, i, :], scales[i]).then_inc(consts2, DMA)
            sp.dma_start(sc3[:], scales[4]).then_inc(consts2, DMA)

            def load(dst, c, signal):
                for n in range(NB):
                    sp.dma_start(dst[:, n * BLK:(n + 1) * BLK, :], x1_c[c, :, n, :, :]).then_inc(signal, DMA)

            load(x_in, 0, xin_landed)

            def step(c, s):
                if live(c - 2, CHUNKS):
                    wait_apart(sp, out_done, c - 1, passed["sp"])
                    for n in range(NB):
                        sp.dma_start(out_c[c - 2, :, n, :, :], y_out[:, n * BLK:(n + 1) * BLK, :]).then_inc(out_stored, DMA)
                if live(c - 1, CHUNKS):
                    wait_apart(sp, res_done, c - 1, passed["sp"])
                    load(x_res, c - 1, xres_landed)
                if live(c + 3, CHUNKS):
                    wait_apart(sp, xT_done, c + 3, passed["sp"])
                    load(x_in, c + 3, xin_landed)

            drive(sp, step, **STEPS)
            sp.wait_ge(out_done, CHUNKS)
            for n in range(NB):
                sp.dma_start(out_c[CHUNKS - 1, :, n, :, :], y_out[:, n * BLK:(n + 1) * BLK, :]).then_inc(out_stored, DMA)
            sp.wait_ge(out_stored, CHUNKS * NB * DMA)

        @block.tensor
        def _(pe):
            def product(ps, o, wh, wl, ah, al, kt, ready=None):
                for k in range(kt):
                    if ready is not None:
                        ready(k)
                    w_hi = wh[:, k, o * P:(o + 1) * P]
                    a_hi, a_lo = (ah[:, k, :], al[:, k, :]) if kt > 1 else (ah[:], al[:])
                    pe.matmul(ps[:], w_hi, a_hi, start=(k == 0), stop=False)
                    if wl is not None:
                        pe.matmul(ps[:], wl[:, k, o * P:(o + 1) * P], a_hi, start=False, stop=False)
                    mm = pe.matmul(ps[:], w_hi, a_lo, start=False, stop=(k == kt - 1))
                return mm

            def step(c, s, lows):
                if live(c, CHUNKS):
                    for o in range(KT):
                        wait(pe, gelu3_done, (c - 1) * KT + o + 1)
                        ready = (lambda k: wait(pe, g1_lo, c * KT + k + 1)) if o == 0 else None
                        product(ps_r[o], o, h1h, lows["h1"], g1h, g1l, KT, ready).then_inc(l2_done, 1)
                if live(c - 1, CHUNKS):
                    wait(pe, res_done, c - 1)
                    product(ps_y, 0, w3h, lows["w3"], g3h, g3l, KT,
                            lambda k: wait(pe, g3_lo, (c - 1) * KT + k + 1)).then_inc(l4_done, 1)
                if live(c + 1, CHUNKS):
                    wait(pe, x_lo, c + 2)
                    for o in range(KT):
                        wait(pe, silu_done, (c + 1) * KT + o - 1)
                        product(ps_s[o % 2], o, w1h, lows["w1"], xh, xl, 1).then_inc(silu_in, 1)
                        if live(c, CHUNKS):
                            wait(pe, gelu2_done, c * KT + o + 1)
                        product(ps_r[o], o, w2h, lows["w2"], xh, xl, 1).then_inc(up_in, 1)
                if live(c + 2, CHUNKS):
                    wait(pe, xin_landed, (c + 3) * NB * DMA)
                    wait(pe, x_lo, c + 2)
                    if isinstance(c, int) and c == FIRST:
                        pe.wait_ge(consts2, 6 * DMA)
                    for a in range(CB):
                        mm = pe.transpose(ps_x[:, a * P:(a + 1) * P], x_in[:, a, :], id_sb[:])
                    mm.then_inc(xT_done, 1)
                if live(c - 1, CHUNKS):
                    wait(pe, y_copied, c)
                    for a in range(CB):
                        mm = pe.transpose(ps_y[:, a * P:(a + 1) * P], y_sb[:, a * P:(a + 1) * P], id_sb[:])
                    mm.then_inc(y_turned, 1)
                if live(c, CHUNKS):
                    for o in range(KT):
                        if live(c + 1, CHUNKS):
                            wait(pe, gate_done, (c + 1) * KT + o + 1)
                        else:
                            wait(pe, gelu2_done, c * KT + o + 1)
                        ready = (lambda k: wait(pe, g2_lo, c * KT + k + 1)) if o == 0 else None
                        product(ps_r[o], o, h2h, lows["h2"], g2h, g2l, KT, ready).then_inc(l3_done, 1)

            pe.wait_ge(ones_set, 1)
            pe.wait_ge(lo_marked, 1)
            pe.matmul(ps_y[:, 0:N_PIECES], ones[:], has_lo[:], start=True, stop=True).then_inc(lo_counted, 1)
            pe.wait_ge(flag_set, 1)
            any_lo = pe.value_load(flag[:].bitcast(mybir.dt.int32))
            weight_lows = {"w1": w1l, "w2": w2l, "h1": h1l, "h2": h2l, "w3": w3l}
            with pe.If(any_lo != 0):
                drive(pe, lambda c, s: step(c, s, weight_lows), **STEPS)
            with pe.Else():
                drive(pe, lambda c, s: step(c, s, dict.fromkeys(weight_lows)), **STEPS)

        @block.scalar
        def _(act):
            def gelus(c, layer, in_done, out_hi, prev_use, lo_done, done):
                for o in range(KT):
                    wait(act, in_done, c * KT + o + 1)
                    wait(act, lo_done, c * KT + o - 1)
                    if o == 0 and prev_use is not None:
                        wait(act, *prev_use)
                    scale = sc[:, 2 + layer, o:o + 1]
                    nc.scalar.activation(gelu_f[:, o % 2, :], ps_r[o][:], ACT.Gelu, scale=scale)
                    nc.scalar.activation(out_hi[:, o, :], ps_r[o][:], ACT.Gelu, scale=scale).then_inc(done, 1)

            def step(c, s):
                if live(c, CHUNKS):
                    wait(act, g3_lo, c * KT)
                    gelus(c, 0, l2_done, g2h, (l3_done, c * KT), g2_lo, gelu2_done)
                if live(c - 1, CHUNKS):
                    wait(act, l4_done, c)
                    wait(act, y_turned, c - 1)
                    nc.scalar.activation(y_sb[:], ps_y[:], ACT.Copy, scale=sc3[:, 0:1]).then_inc(y_copied, 1)
                if live(c + 1, CHUNKS):
                    for o in range(KT):
                        wait(act, silu_in, (c + 1) * KT + o + 1)
                        wait(act, gate_done, (c + 1) * KT + o - 1)
                        nc.scalar.activation(act_f[:, o % 2, :], ps_s[o % 2][:], ACT.Silu,
                                             scale=sc[:, 0, o:o + 1]).then_inc(silu_done, 1)
                if live(c + 2, CHUNKS):
                    wait(act, xT_done, c + 3)
                    wait(act, up_in, (c + 2) * KT)
                    nc.scalar.activation(xh[:], ps_x[:], ACT.Copy).then_inc(x_hi, 1)
                if live(c, CHUNKS):
                    wait(act, g2_lo, (c + 1) * KT)
                    gelus(c, 1, l3_done, g3h, (l4_done, c), g3_lo, gelu3_done)

            act.wait_ge(consts2, 6 * DMA)
            drive(act, step, **STEPS)

        @block.vector
        def _(dve):
            def lows(c, hi, lo, done, signal):
                for o in range(KT):
                    wait(dve, done, c * KT + o + 1)
                    nc.vector.tensor_tensor(lo[:, o, :], gelu_f[:, o % 2, :], hi[:, o, :].bitcast(F32),
                                            ALU.subtract).then_inc(signal, 1)

            def step(c, s):
                if live(c, CHUNKS):
                    lows(c, g2h, g2l, gelu2_done, g2_lo)
                if live(c + 1, CHUNKS):
                    wait(dve, l2_done, (c + 1) * KT)
                    for o in range(KT):
                        n = (c + 1) * KT + o + 1
                        wait(dve, silu_done, n)
                        wait(dve, up_in, n)
                        nc.vector.scalar_tensor_tensor(out=gate_f[:, o % 2, :], in0=ps_r[o][:], scalar=sc[:, 1, o:o + 1],
                                                       in1=act_f[:, o % 2, :], op0=ALU.mult,
                                                       op1=ALU.mult).then_inc(gate_done, 1)
                        wait(dve, gate_done, n)
                        nc.vector.tensor_copy(g1h[:, o, :], gate_f[:, o % 2, :]).then_inc(g1_hi, 1)
                        wait(dve, g1_hi, n)
                        nc.vector.tensor_tensor(g1l[:, o, :], gate_f[:, o % 2, :], g1h[:, o, :].bitcast(F32),
                                                ALU.subtract).then_inc(g1_lo, 1)
                if live(c + 2, CHUNKS):
                    wait(dve, x_hi, c + 3)
                    nc.vector.tensor_tensor(xl[:], ps_x[:], xh[:].bitcast(F32), ALU.subtract).then_inc(x_lo, 1)
                if live(c - 1, CHUNKS):
                    wait(dve, y_turned, c)
                    wait(dve, xres_landed, c * NB * DMA)
                    wait(dve, out_done, c - 1)
                    nc.vector.tensor_tensor(res[:].rearrange("p a d -> p (a d)"), ps_y[:],
                                            x_res[:].rearrange("p a d -> p (a d)"), ALU.add).then_inc(res_done, 1)
                    wait(dve, res_done, c)
                    for a in range(CB):
                        nc.vector.bn_stats(bn6[:, a, :], res[:, a, :]).then_inc(bn_done, 1)
                    wait_apart(dve, bn_done, c * CB, passed["dve"])
                    for a in range(CB):
                        nc.vector.bn_aggr(meanvar[:, a, :], bn6[:, a, :]).then_inc(stats_done, 1)
                if live(c, CHUNKS):
                    lows(c, g3h, g3l, gelu3_done, g3_lo)

            nc.vector.tensor_scalar(has_lo[:], lo_max[:], 0.0, None, ALU.not_equal).then_inc(lo_marked, 1)
            dve.wait_ge(lo_counted, 1)
            nc.vector.tensor_reduce(flag[:], ps_y[0:1, 0:N_PIECES], AX_X, ALU.max).then_inc(flag_set, 1)
            drive(dve, step, **STEPS)

        @block.gpsimd
        def _(pool):
            nc.gpsimd.memset(ones[:], 1.0).then_inc(ones_set, 1)
            nc.gpsimd.memset(minus_half[:], -0.5).then_inc(eps_done, 1)

            def step(c, s):
                if live(c - 1, CHUNKS):
                    wait_apart(pool, stats_done, c * CB, passed["pool"])
                    nc.gpsimd.tensor_scalar(vareps[:], meanvar[:, :, 1], EPS, None, ALU.add).then_inc(eps_done, 1)
                    wait(pool, eps_done, c + 1)
                    nc.gpsimd.tensor_tensor(rstd[:], vareps[:], minus_half[:], ALU.pow).then_inc(rstd_done, 1)
                    wait(pool, rstd_done, c)
                    wait_apart(pool, out_stored, (c - 1) * NB * DMA, passed["pool"])
                    for a in range(CB):
                        ins = nc.gpsimd.tensor_scalar(y_out[:, a, :], res[:, a, :], meanvar[:, a, 0:1],
                                                      rstd[:, a:a + 1], ALU.subtract, ALU.mult)
                    ins.then_inc(out_done, 1)

            drive(pool, step, **STEPS)


def build(nc, a, out):
    x1_dram = nc.dram_tensor("x1_scratch", [BATCH, P, BLK, D], F32, kind="Internal").ap()
    qk_dram = nc.dram_tensor("qk_scratch", [2, 2, 3, DH, HEADS, SEQ], F32, kind="Internal").ap()
    with ExitStack() as ctx:
        wts = []
        for name, kt, n in (("w1", 1, HID), ("w2", 1, HID), ("h1", KT, HID), ("h2", KT, HID), ("w3", KT, D)):
            wts.append(tuple(ctx.enter_context(nc.sbuf_tensor(f"{name}_{part}", [P, kt, n], F32R)) for part in ("hi", "lo")))
        lo_max = ctx.enter_context(nc.sbuf_tensor("lo_max", [P, N_PIECES], F32))
        raw_w = [a[n].rearrange("(k p) n -> p k n", p=P) for n in ("w1T", "w2T", "h1T", "h2T", "w3T")]
        attention(nc, wts, a["x"], a["xT"], a["wqT"], a["wkT"], a["wvT"], a["woT"], a["bo"], a["qscale"], a["ident"],
                  a["corner"], a["rows"], x1_dram, qk_dram, raw_w, lo_max)
        scales = [a[n] for n in ("w1_s", "w2_s", "h1_s", "h2_s", "w3_s")]
        ffn(nc, wts, scales, a["ident"], x1_dram, out, lo_max)


def bias_rows():
    pos = np.arange(SEQ, dtype=np.float32)
    local = pos % P
    first = (pos < P).astype(np.float32)
    second = 1.0 - first
    sign = first - second
    one = np.ones_like(pos)
    pairs = [(sign * pos, one), (-sign, pos), (-2.0 * pos * first, first), (second, -2.0 * local * second)]
    for block in (first, second):
        for t in range(1, STEPS_T + 1):
            pairs.append((block * (local >= t), 2.0 * block * (local >= t)))
    rows = np.zeros((P, 2, SEQ), np.float32)
    for r, (query, key) in enumerate(pairs):
        rows[STACK + r, 0], rows[STACK + r, 1] = query, key
    rows[MROW:, 1] = 1.0
    return rows


def shape_constants():
    i = np.arange(CORNER, dtype=np.float32)
    corner = np.zeros((P, CORNER), np.float32)
    corner[STEPS_T:, :] = 2.0 * np.minimum(i[:, None], i[None, :])
    qscale = np.tile(1.0 / (np.array(slopes()) * np.sqrt(float(DH))), DH).astype(np.float32)
    return {
        "qscale": qscale.reshape(P, 1),
        "ident": np.eye(P, dtype=np.float32),
        "corner": corner,
        "rows": bias_rows(),
    }


def by_feature(w):
    return w.reshape(HEADS, DH, D).transpose(1, 0, 2).reshape(D, D).T


def kernel(**inputs):
    import concourse.bacc as bacc
    from concourse.bass_utils import run_bass_kernel_spmd

    x = inputs["L0_attn_x"]
    laid = {
        "x": x, "xT": x.transpose(0, 2, 1),
        "wqT": by_feature(inputs["L0_attn_wq"]), "wkT": by_feature(inputs["L0_attn_wk"]), "wvT": inputs["L0_attn_wv"].T,
        "woT": inputs["L0_attn_wo"].T, "bo": np.broadcast_to(inputs["L0_attn_bo"], (P, D)),
        "w1T": inputs["L0_ffn_w1_w"].T, "w2T": inputs["L0_ffn_w2_w"].T, "h1T": inputs["L0_ffn_h1_w"].T,
        "h2T": inputs["L0_ffn_h2_w"].T, "w3T": inputs["L0_ffn_w3_w"].T,
        **{f"{n}_s": inputs[f"L0_ffn_{n}_s"].reshape(-1, P).T for n in ("w1", "w2", "h1", "h2", "w3")},
        **shape_constants(),
    }
    nc = bacc.Bacc("TRN2", target_bir_lowering=False, num_devices=1)
    arrays, operands = {}, {}
    for name, value in laid.items():
        value = np.ascontiguousarray(value)
        arrays[f"in_{name}"] = value
        operands[name] = nc.dram_tensor(f"in_{name}", value.shape, mybir.dt.from_np(value.dtype), kind="ExternalInput").ap()
    out = nc.dram_tensor("out_0", (BATCH, SEQ, D), F32, kind="ExternalOutput").ap()
    build(nc, operands, out)
    r = run_bass_kernel_spmd(nc, [arrays], core_ids=[0])
    return r.results[0]["out_0"]
```

```python
from contextlib import ExitStack

import numpy as np

import concourse.bass as bass
from concourse import mybir

F32 = mybir.dt.float32
F32R = mybir.dt.float32r
BF16 = mybir.dt.bfloat16
ACT = mybir.ActivationFunctionType
ALU = mybir.AluOpType
AX_X = mybir.AxisListType.X
AX_XY = mybir.AxisListType.XY

P = 128
BATCH = 32
SEQ = 256
D = 128
HEADS = 16
DH = D // HEADS
BLK = SEQ // P
HALF = HEADS // 2
GROUP = 4
VCOLS = 32
HID = 512
KT = HID // P
CHUNK = 512
CB = CHUNK // P
CHUNKS = BATCH * SEQ // CHUNK
EPS = 1e-5
RAW_BUFS = 4
N_PIECES = 11
DMA = 16

STACK = 3 * DH
MROW = P - 2
KA = MROW
STEPS_T = (MROW - STACK - 4) // BLK
CORNER = P - STEPS_T
F32_MAX = float(np.finfo(np.float32).max)
QH, QL, KH, KL = range(4)


def slopes():
    start = 2.0 ** (-2.0 ** (-(np.log2(HEADS) - 3)))
    return [float(np.float32(start * start ** i)) for i in range(HEADS)]


def wait(eng, sem, value):
    if not isinstance(value, int) or value > 0:
        eng.wait_ge(sem, value)


def wait_apart(eng, sem, value, passed):
    wait(eng, sem, value)
    if not isinstance(value, int):
        eng.sem_inc(passed, 1)


PV_AT = (5, 9, 13)
PE_AT = {"last pv": 1, "turn max 1": 1, "v": 2, "qk": 4, "turn o 0": 6, "turn o 1": 7, "turn max 0": 9, "turn norm": 10, "wo": 12}
ACT_AT = {"max hi 1": 1, "copy o 1": 2, "v": 3, "qk hi": 4, "max hi 0": 9, "oT": 10, "copy o 0": 11}
DVE_AT = {"max lo 1": 1, "qk lo": 4, "norm": (7, 8), "max lo 0": 10, "res": 13, "stats": 14}
A_BANK = [1 if h == 3 else (h - 4) % HEADS % 3 for h in range(HEADS)]


def a_released(b, h):
    before = [g for g in range(h - HEADS, h) if A_BANK[g % HEADS] == A_BANK[h]][-1]
    return b * HEADS + before + 1


def live(index, count):
    return not isinstance(index, int) or 0 <= index < count


def drive(eng, step, first, loop_from, loop_to, last, unroll):
    for t in range(first, loop_from):
        step(t, t % 2)
    with eng.Fori(0, (loop_to - loop_from) // unroll, 1) as i:
        for u in range(unroll):
            step(i * unroll + (loop_from + u), (loop_from + u) % 2)
    for t in range(loop_to, last + 1):
        step(t, t % 2)


class Carried:

    def __init__(self, nc, ctx):
        def sb(name, shape, dt=F32):
            return ctx.enter_context(nc.sbuf_tensor(name, shape, dt))

        def sem(name):
            return ctx.enter_context(nc.semaphore(name))

        self.id_sb = sb("id_sb", [P, P])
        self.minus_half = sb("minus_half", [P, CB])
        self.x_in = sb("x_in", [P, CB, D])
        self.x_parts = sb("x_parts", [P, 2, CHUNK], F32R)
        self.sc = sb("sc", [P, 4, KT])
        self.sc3 = sb("sc3", [P, 1])
        self.lo_max = sb("lo_max", [P, N_PIECES])
        self.has_lo = sb("has_lo", [P, N_PIECES])
        self.flag = sb("flag", [1, 1])
        self.res = [sb(f"res{i}", [P, BLK, D]) for i in range(2)]
        self.meanvar = [sb(f"meanvar{i}", [P, BLK, 2]) for i in range(2)]
        self.vareps = sb("vareps", [P, BLK])
        self.rstd = sb("rstd", [P, BLK])
        self.x1_sb = [sb(f"x1_sb{i}", [P, BLK, D]) for i in range(2)]
        self.xin_landed, self.scales_landed = sem("xin_landed"), sem("scales_landed")
        self.xT_done, self.x_hi, self.x_lo = sem("xT_done"), sem("x_hi"), sem("x_lo")
        self.flag_set, self.stats_done = sem("flag_set"), sem("stats_done")
        self.eps_done, self.rstd_done = sem("eps_done"), sem("rstd_done")
        self.x1_done, self.x1_stored = sem("x1_done"), sem("x1_stored")


def norm_x1(nc, pool, b, par, carried, passed):
    mv = carried.meanvar[par]
    vareps, rstd = carried.vareps, carried.rstd
    wait_apart(pool, carried.stats_done, (b + 1) * BLK, passed)
    nc.gpsimd.tensor_scalar(vareps[:], mv[:, :, 1], EPS, None, ALU.add).then_inc(carried.eps_done, 1)
    wait(pool, carried.eps_done, b + 2)
    nc.gpsimd.tensor_tensor(rstd[:], vareps[:], carried.minus_half[:, 0:BLK], ALU.pow).then_inc(carried.rstd_done, 1)
    wait(pool, carried.rstd_done, b + 1)
    wait_apart(pool, carried.x1_stored, (b - 1) * DMA, passed)
    for a in range(BLK):
        ins = nc.gpsimd.tensor_scalar(carried.x1_sb[par][:, a, :], carried.res[par][:, a, :], mv[:, a, 0:1],
                                      rstd[:, a:a + 1], ALU.subtract, ALU.mult)
    ins.then_inc(carried.x1_done, 1)


def load_chunk(sp, x1_dram, c, dst, signal):
    for n in range(CHUNK // SEQ):
        sp.dma_start(dst[:, n * BLK:(n + 1) * BLK, :],
                     x1_dram.rearrange("(c n) p a d -> c p n a d", n=CHUNK // SEQ)[c, :, n, :, :]).then_inc(signal, DMA)


def attention(nc, wts, x, xT, wqT, wkT, wvT, woT, bo, qscale, ident, corner, rows, x1_dram, qk_dram, raw_w, scales,
              carried):
    slope = slopes()
    with ExitStack() as ctx:
        def sb(name, shape, dt=F32):
            return ctx.enter_context(nc.sbuf_tensor(name, shape, dt))

        def sem(name):
            return ctx.enter_context(nc.semaphore(name))

        id_sb, res, meanvar, x1_sb, lo_max, has_lo = (carried.id_sb, carried.res, carried.meanvar, carried.x1_sb,
                                                      carried.lo_max, carried.has_lo)
        rows_sb = carried.x_in.rearrange("p a d -> p (a d)").rearrange("p (n t) -> p n t", n=2)
        qk_sb = carried.x_parts.rearrange("p n (b t) -> p (n b) t", b=2)
        stats_done, x1_done, x1_stored = carried.stats_done, carried.x1_done, carried.x1_stored
        wq_sb, wk_sb, wv_sb, wo_sb = (sb(n, [P, D]) for n in ("wq_sb", "wk_sb", "wv_sb", "wo_sb"))
        bo_sb = sb("bo_sb", [P, D])
        qscale_sb = sb("qscale_sb", [P, 1])
        idb_sb = sb("idb_sb", [P, P], BF16)
        corner_f = sb("corner_f", [P, CORNER])
        corner_sb = sb("corner_sb", [P, BLK, CORNER], BF16)
        qk_stack = [sb(f"qk_stack{i}", [P, 2, HEADS, SEQ], F32R) for i in range(2)]
        q_stack, k_stack = ([tile[:, n, :, :] for tile in qk_stack] for n in range(2))
        probs = sb("probs", [P, HALF, BLK * SEQ])
        v_aug = [sb(f"v_aug{i}", [P, BLK, HEADS, VCOLS]) for i in range(2)]
        xT_sb = [sb(f"xT_sb{i}", [P, SEQ]) for i in range(2)]
        scored = sb("scored", [P, 2, BLK, SEQ])
        x_sb = [sb(f"x_sb{i}", [P, BLK, D]) for i in range(2)]
        xb_sb = [sb(f"xb_sb{i}", [P, BLK, D]) for i in range(2)]
        corner_rows = sb("corner_rows", [P, BLK, SEQ])
        negmax = sb("negmax", [P, 2, HALF, BLK])
        mrow_hi = [sb(f"mrow_hi{i}", [BLK * HALF, P], F32R) for i in range(2)]
        mrow_lo = [sb(f"mrow_lo{i}", [BLK * HALF, P], F32R) for i in range(2)]
        o_sb = sb("o_sb", [P, HEADS // GROUP, SEQ])
        recip = sb("recip", [P, BLK, HEADS])
        o_norm = sb("o_norm", [P, BLK, D])
        oT_sb = sb("oT_sb", [P, SEQ])
        bn6 = sb("bn6", [P, BLK, 6])
        ones = sb("ones", [P, VCOLS])
        raw = sb("raw", [P, RAW_BUFS, HID])

        ps_a = [ctx.enter_context(nc.psum_tensor(f"ps_a{i}", [P, 512], F32)) for i in range(3)]
        ps_b = [ctx.enter_context(nc.psum_tensor(f"ps_b{i}", [P, 512], F32)) for i in range(2)]
        ps_o = ctx.enter_context(nc.psum_tensor("ps_o", [P, 2, SEQ], F32))
        ps_m = [ctx.enter_context(nc.psum_tensor(f"ps_m{i}", [P, 512], F32)) for i in range(2)]

        passed = {e: sem(f"passed_{e}") for e in ("sp", "dve", "pool")}
        qk_const_landed = sem("qk_const_landed")
        const_landed = sem("const_landed")
        const_set = sem("const_set")
        rows_landed = sem("rows_landed")
        rows_laid = [sem(f"rows_laid{i}") for i in range(2)]
        v_laid = sem("v_laid")
        xT_landed, x_landed = sem("xT_landed"), sem("x_landed")
        qk_done, qk_hi, qk_lo = sem("qk_done"), sem("qk_hi"), sem("qk_lo")
        spilled = sem("spilled")
        corner_zero, corner_laid = sem("corner_zero"), sem("corner_laid")
        stacked = [sem(f"stacked{i}") for i in range(2)]
        v_done, v_copied = sem("v_done"), sem("v_copied")
        scores_a, max_done = sem("scores_a"), sem("max_done")
        mT_done, m_hi, m_lo = sem("mT_done"), sem("m_hi"), sem("m_lo")
        m_landed = [sem(f"m_landed{i}") for i in range(2)]
        scores_b, exp_done = sem("scores_b"), sem("exp_done")
        pv_done, o_copied = sem("pv_done"), sem("o_copied")
        o_turned, recip_done, normed = sem("o_turned"), sem("recip_done"), sem("normed")
        oT_done, oT_copied = sem("oT_done"), sem("oT_copied")
        wo_done, res_done = sem("wo_done"), sem("res_done")
        bn_done, xb_done = sem("bn_done"), sem("xb_done")
        ones_set, lo_marked, lo_counted = sem("ones_set"), sem("lo_marked"), sem("lo_counted")
        raw_landed, raw_split = [sem(f"raw_landed{i}") for i in range(RAW_BUFS)], sem("raw_split")
        raw_hi, lo_seen = sem("raw_hi"), sem("lo_seen")

        pieces = []
        for (hi, lo), src in zip(wts, raw_w):
            kt, n = src.shape[1:]
            for a in range(0, kt, HID // n):
                pieces.append(tuple(w[:, a:a + HID // n, :] for w in (hi, lo, src)))
        piece_at = [(-2, 8)] * RAW_BUFS + [(0, 11), (1, 11), (2, 11), (BATCH - 3, 11), (BATCH - 2, 11),
                                           (BATCH - 1, 4), (BATCH - 1, 10)]
        assert len(pieces) == N_PIECES == len(piece_at)

        def pieces_of(t, k):
            return [n for n, (step, head) in enumerate(piece_at) if step == t and k in (None, head)]

        def raw_piece(n):
            width = pieces[n][2].shape[2]
            return raw[:, n % RAW_BUFS, :].rearrange("p (k n) -> p k n", n=width)

        N_CONST, N_QK_CONST = 5, 3

        STEPS = dict(first=-2, loop_from=3, loop_to=BATCH - 3, last=BATCH, unroll=2)
        FIRST = STEPS["first"]

        block = ctx.enter_context(nc.Block())

        @block.sync
        def _(sp):
            sp.dma_start(xT_sb[0][:], xT[0]).then_inc(xT_landed, DMA)
            sp.dma_start(rows_sb, rows).then_inc(rows_landed, DMA)
            for dst, src in ((wq_sb, wqT), (wk_sb, wkT), (qscale_sb, qscale)):
                sp.dma_start(dst[:], src).then_inc(qk_const_landed, DMA)
            for dst, src in ((id_sb, ident), (corner_f, corner), (wv_sb, wvT), (wo_sb, woT), (bo_sb, bo)):
                sp.dma_start(dst[:], src).then_inc(const_landed, DMA)
            sp.wait_ge(xT_landed, DMA)
            sp.dma_start(xT_sb[1][:], xT[1]).then_inc(xT_landed, DMA)
            sp.dma_start(x_sb[0][:], x[0].rearrange("(a p) d -> p a d", p=P)).then_inc(x_landed, DMA)

            def stack(b, par, hf):
                heads = slice(hf * HALF, (hf + 1) * HALF)
                sp.dma_start(qk_stack[par][0:STACK, :, heads, :].bitcast(F32),
                             qk_dram[par, :, :, :, heads, :].rearrange("n r d h t -> (r d) n h t")).then_inc(stacked[hf], DMA)

            def spill(par):
                src = qk_sb.bitcast(F32)
                flat = qk_dram[par].rearrange("n r d h t -> (d h) (n r) t")
                sp.dma_start(flat[:, 1:5, :], src).then_inc(spilled, DMA)
                sp.dma_start(flat[:, 0:6:5, :], src[:, QH:KL:KH, :]).then_inc(spilled, DMA)

            def max_rows(b, par, hf):
                wait_apart(sp, m_lo, b * 2 + hf + 1, passed["sp"])
                for r, src in enumerate((mrow_hi[hf], mrow_lo[hf])):
                    dst = q_stack[par][MROW + r:MROW + r + 1, hf * HALF:(hf + 1) * HALF, :]
                    sp.dma_start(dst.bitcast(F32).rearrange("p h (b q) -> p (h b) q", b=BLK),
                                 src[:].bitcast(F32)).then_inc(m_landed[hf], DMA)

            def step(t, s):
                if live(t + 1, BATCH):
                    wait_apart(sp, spilled, (t + 2) * 2 * DMA, passed["sp"])
                    wait_apart(sp, scores_b, t * HEADS, passed["sp"])
                    stack(t + 1, 1 - s, 1)
                if live(t, BATCH):
                    max_rows(t, s, 1)
                if live(t - 2, BATCH):
                    wait_apart(sp, x1_done, t - 1, passed["sp"])
                    wait_apart(sp, x1_stored, (t - 2) * DMA, passed["sp"])
                    sp.dma_start(x1_dram[t - 2], x1_sb[s][:]).then_inc(x1_stored, DMA)
                if live(t + 3, BATCH) and live(t + 1, BATCH):
                    wait_apart(sp, v_done, t + 2, passed["sp"])
                    wait_apart(sp, xT_landed, (t + 3) * DMA, passed["sp"])
                    sp.dma_start(xT_sb[1 - s][:], xT[t + 3]).then_inc(xT_landed, DMA)
                if live(t + 2, BATCH):
                    wait_apart(sp, qk_lo, (t + 2) * 2 + 2, passed["sp"])
                    if live(t, BATCH):
                        wait_apart(sp, stacked[0], (t + 1) * DMA, passed["sp"])
                        wait_apart(sp, stacked[1], (t + 1) * DMA, passed["sp"])
                    spill(s)
                    wait_apart(sp, spilled, (t + 3) * 2 * DMA, passed["sp"])
                    if live(t, BATCH):
                        wait_apart(sp, scores_b, t * HEADS + HALF, passed["sp"])
                    if isinstance(t, int) and t < 0:
                        sp.wait_ge(rows_laid[s], 3)
                    stack(t + 2, s, 0)
                if live(t + 1, BATCH):
                    max_rows(t + 1, 1 - s, 0)
                if live(t + 1, BATCH) and live(t, BATCH):
                    wait_apart(sp, xb_done, t, passed["sp"])
                    wait_apart(sp, x_landed, (t + 1) * DMA, passed["sp"])
                    sp.dma_start(x_sb[1 - s][:], x[t + 1].rearrange("(a p) d -> p a d", p=P)).then_inc(x_landed, DMA)

                if isinstance(t, int) and t == BATCH - 2:
                    for i in range(4):
                        sp.dma_start(carried.sc[:, i, :], scales[i]).then_inc(carried.scales_landed, DMA)
                    sp.dma_start(carried.sc3[:], scales[4]).then_inc(carried.scales_landed, DMA)
                    load_chunk(sp, x1_dram, 0, carried.x_in, carried.xin_landed)
                if isinstance(t, int) and t == BATCH:
                    sp.wait_ge(carried.xT_done, 1)
                    load_chunk(sp, x1_dram, 1, carried.x_in, carried.xin_landed)

            drive(sp, step, **STEPS)
            sp.wait_ge(x1_stored, (BATCH - 1) * DMA)

        @block.tensor
        def _(pe):
            def add_corner(ps):
                out = ps[:].rearrange("p (b c) -> p b c", c=P)[:, 0:4:3, STEPS_T:P]
                return pe.matmul(out, idb_sb[:], corner_sb[:], start=False, stop=True, skip_group_check=True)

            def score_max(b, par, h):
                if h % HALF == 0:
                    wait(pe, stacked[h // HALF], (b + 1) * DMA)
                wait(pe, max_done, a_released(b, h))
                ps = ps_a[A_BANK[h]]
                for qb in range(BLK):
                    mm = pe.matmul(ps[:, qb * SEQ:(qb + 1) * SEQ], q_stack[par][0:KA, h, qb * P:(qb + 1) * P],
                              k_stack[par][0:KA, h, :], start=(qb == 0), stop=True,
                              skip_group_check=True)
                mm.then_inc(scores_a, 1)

            def score_exp(b, par, h):
                if h % HALF == 0:
                    wait(pe, m_landed[h // HALF], (b + 1) * 2 * DMA)
                wait(pe, exp_done, b * HEADS + h - 1)
                ps = ps_b[h % 2]
                for kb in range(BLK):
                    pe.matmul(ps[:, kb * SEQ:(kb + 1) * SEQ], k_stack[par][:, h, kb * P:(kb + 1) * P],
                              q_stack[par][:, h, :], start=(kb == 0), stop=False, skip_group_check=True)

            def pv(b, par, j):
                if j == 0:
                    wait(pe, v_copied, b + 1)
                wait(pe, exp_done, b * HEADS + GROUP * (j + 1))
                if j % 2 == 0:
                    wait(pe, o_copied, b * 2 + j // 2)
                for kb in range(BLK):
                    for g in range(GROUP):
                        h = j * GROUP + g
                        mm = pe.matmul(ps_o[VCOLS * g:VCOLS * (g + 1), j % 2, :],
                                       v_aug[par][:, kb, h, :], probs[:, h % HALF, kb * SEQ:(kb + 1) * SEQ],
                                       start=(kb == 0), stop=(kb == BLK - 1), skip_group_check=True)
                mm.then_inc(pv_done, 1)

            def turn_max(b, hf):
                wait(pe, max_done, b * HEADS + (hf + 1) * HALF)
                pe.transpose(ps_m[0][0:BLK * HALF, 0:P], negmax[:, hf, :, :].rearrange("p h a -> p (h a)"),
                             id_sb[:]).then_inc(mT_done, 1)

            def turn_o(b, qb):
                wait(pe, o_copied, b * 2 + 2)
                for j in range(HEADS // GROUP):
                    mm = pe.transpose(ps_m[qb][:, j * P:(j + 1) * P], o_sb[:, j, qb * P:(qb + 1) * P], id_sb[:])
                mm.then_inc(o_turned, 1)

            def step(t, s):
                if isinstance(t, int) and t == FIRST + 1:
                    pe.wait_ge(const_landed, N_CONST * DMA)
                    pe.wait_ge(const_set, 2)
                if isinstance(t, int) and t == BATCH:
                    pe.wait_ge(carried.xin_landed, CHUNK // SEQ * DMA)
                    pe.wait_ge(max_done, BATCH * HEADS)
                    for a in range(CB):
                        mm = pe.transpose(ps_a[0][:, a * P:(a + 1) * P], carried.x_in[:, a, :], id_sb[:])
                    mm.then_inc(carried.xT_done, 1)
                for k in range(HEADS):
                    if live(t + 1, BATCH):
                        score_max(t + 1, 1 - s, k)
                    if live(t, BATCH):
                        score_exp(t, s, k)
                    if live(t, BATCH):
                        add_corner(ps_b[k % 2]).then_inc(scores_b, 1)
                        if k in PV_AT:
                            pv(t, s, PV_AT.index(k))
                    if k == PE_AT["last pv"] and live(t - 1, BATCH):
                        pv(t - 1, 1 - s, 3)
                    if k == PE_AT["turn max 1"] and live(t, BATCH):
                        wait(pe, m_lo, t * 2 + 1)
                        turn_max(t, 1)
                    if k == PE_AT["v"] and live(t + 1, BATCH):
                        wait(pe, xT_landed, (t + 2) * DMA)
                        if live(t - 2, BATCH):
                            wait(pe, res_done, t - 1)
                        elif live(t, BATCH):
                            wait(pe, v_copied, t + 1)
                        for tb in range(BLK):
                            mm = pe.matmul(ps_m[1][:, tb * D:(tb + 1) * D], xT_sb[1 - s][:, tb * P:(tb + 1) * P], wv_sb[:],
                                           start=True, stop=True)
                        mm.then_inc(v_done, 1)
                    if k == PE_AT["qk"] and live(t + 2, BATCH):
                        wait(pe, xT_landed, (t + 3) * DMA)
                        if live(t, BATCH):
                            wait(pe, m_lo, t * 2 + 2)
                        else:
                            wait(pe, qk_lo, (t + 1) * 2 + 2)
                        if isinstance(t, int) and t == FIRST:
                            pe.wait_ge(qk_const_landed, N_QK_CONST * DMA)
                        for n, w in enumerate((wq_sb, wk_sb)):
                            mm = pe.matmul(ps_m[0][:, n * SEQ:(n + 1) * SEQ], w[:], xT_sb[s][:], start=True, stop=True)
                        mm.then_inc(qk_done, 1)
                    if k == PE_AT["turn o 0"] and live(t - 1, BATCH):
                        if live(t + 2, BATCH):
                            wait(pe, qk_lo, (t + 2) * 2 + 2)
                        elif live(t, BATCH):
                            wait(pe, m_lo, t * 2 + 2)
                        else:
                            wait(pe, normed, (t - 2) * 2 + 1)
                        turn_o(t - 1, 0)
                    if k == PE_AT["turn o 1"] and live(t - 1, BATCH):
                        if live(t + 1, BATCH):
                            wait(pe, v_copied, t + 2)
                        else:
                            wait(pe, res_done, t - 1)
                        turn_o(t - 1, 1)
                    if k == PE_AT["turn norm"] and live(t - 1, BATCH):
                        wait(pe, normed, (t - 1) * 2 + 2)
                        for qb in range(BLK):
                            mm = pe.transpose(ps_m[1][:, qb * P:(qb + 1) * P], o_norm[:, qb, :], id_sb[:])
                        mm.then_inc(oT_done, 1)
                    if k == PE_AT["turn max 0"] and live(t + 1, BATCH):
                        if live(t - 1, BATCH):
                            wait(pe, normed, (t - 1) * 2 + 1)
                        else:
                            wait(pe, qk_lo, (t + 2) * 2 + 2)
                        turn_max(t + 1, 0)
                    if k == PE_AT["wo"] and live(t - 1, BATCH):
                        wait(pe, oT_copied, t)
                        for qb in range(BLK):
                            mm = pe.matmul(ps_m[1][:, qb * D:(qb + 1) * D], oT_sb[:, qb * P:(qb + 1) * P], wo_sb[:],
                                           start=True, stop=True)
                        mm.then_inc(wo_done, 1)

            drive(pe, step, **STEPS)
            pe.wait_ge(ones_set, 1)
            pe.wait_ge(lo_marked, 1)
            pe.wait_ge(exp_done, BATCH * HEADS)
            pe.matmul(ps_b[0][0:VCOLS, 0:N_PIECES], ones[:], has_lo[:], start=True, stop=True).then_inc(lo_counted, 1)

        @block.scalar
        def _(act):
            def max_hi(b, hf):
                wait(act, mT_done, b * 2 + hf + 1)
                wait(act, m_landed[hf], b * 2 * DMA)
                nc.scalar.activation(mrow_hi[hf][:], ps_m[0][0:BLK * HALF, 0:P], ACT.Copy).then_inc(m_hi, 1)

            def copy_o(b, hf):
                wait(act, pv_done, b * 4 + hf * 2 + 2)
                wait(act, o_turned, b * 2)
                nc.scalar.activation(o_sb[:, 2 * hf:2 * hf + 2, :], ps_o[:], ACT.Copy).then_inc(o_copied, 1)

            def lay_rows(i, first, last):
                nc.scalar.activation(qk_stack[i][:, 1, first:last, :],
                                     rows_sb[:, 1, :].unsqueeze(1).broadcast_to([P, last - first, SEQ]),
                                     ACT.Copy).then_inc(rows_laid[i], 1)

            def step(t, s):
                if isinstance(t, int) and t == BATCH:
                    act.wait_ge(carried.xT_done, 1)
                    act.wait_ge(spilled, BATCH * 2 * DMA)
                    nc.scalar.activation(carried.x_parts[:, 0, :], ps_a[0][:], ACT.Copy).then_inc(carried.x_hi, 1)
                for k in range(HEADS):
                    if live(t, BATCH):
                        wait(act, scores_b, t * HEADS + k + 1)
                        if k % GROUP == 0:
                            wait(act, pv_done, t * 4 + k // GROUP - 1)
                        nc.scalar.activation(probs[:, k % HALF, :], ps_b[k % 2][:], ACT.Exp,
                                             scale=slope[k]).then_inc(exp_done, 1)
                    if k == ACT_AT["max hi 1"] and live(t, BATCH):
                        max_hi(t, 1)
                    if k == ACT_AT["copy o 1"] and live(t - 1, BATCH):
                        copy_o(t - 1, 1)
                    if k == ACT_AT["v"] and live(t + 1, BATCH):
                        wait(act, v_done, t + 2)
                        wait(act, pv_done, t * 4)
                        if isinstance(t, int) and t < 1:
                            act.wait_ge(v_laid, 4)
                        nc.scalar.activation(v_aug[1 - s][:, :, :, 0:DH],
                                             ps_m[1][:, 0:BLK * D].rearrange("p (a h d) -> p a h d", a=BLK, d=DH),
                                             ACT.Copy).then_inc(v_copied, 1)
                    if k == ACT_AT["qk hi"] and live(t + 2, BATCH):
                        wait(act, qk_done, t + 3)
                        wait(act, spilled, (t + 2) * 2 * DMA)
                        nc.scalar.activation(qk_sb[:, QH, :], ps_m[0][:, 0:SEQ], ACT.Copy,
                                             scale=qscale_sb[:, 0:1]).then_inc(qk_hi, 1)
                        nc.scalar.activation(qk_sb[:, KH, :], ps_m[0][:, SEQ:2 * SEQ], ACT.Copy).then_inc(qk_hi, 1)
                    if k == ACT_AT["max hi 0"] and live(t + 1, BATCH):
                        max_hi(t + 1, 0)
                    if k == ACT_AT["oT"] and live(t - 1, BATCH):
                        wait(act, oT_done, t)
                        wait(act, wo_done, t - 1)
                        nc.scalar.activation(oT_sb[:], ps_m[1][:, 0:SEQ], ACT.Copy).then_inc(oT_copied, 1)
                    if k == ACT_AT["copy o 0"] and live(t, BATCH):
                        copy_o(t, 0)
                    if isinstance(t, int):
                        for n in pieces_of(t, k):
                            act.wait_ge(raw_landed[n % RAW_BUFS], (n // RAW_BUFS + 1) * DMA)
                            nc.scalar.activation(pieces[n][0], raw_piece(n), ACT.Copy).then_inc(raw_hi, 1)
                    if isinstance(t, int) and t == FIRST and k == 5:
                        lay_rows(0, HALF, HEADS)
                    if isinstance(t, int) and t == FIRST and k == 15:
                        lay_rows(1, 0, HALF)
                        lay_rows(1, HALF, HEADS)

            act.wait_ge(rows_landed, DMA)
            lay_rows(0, 0, HALF)
            act.wait_ge(qk_const_landed, N_QK_CONST * DMA)
            drive(act, step, **STEPS)

        @block.vector
        def _(dve):
            def lay_rows(i):
                nc.vector.tensor_copy(qk_stack[i][:, 0, :, :], rows_sb[:, 0, :].unsqueeze(1).broadcast_to([P, HEADS, SEQ])
                                      ).then_inc(rows_laid[i], 1)

            def lay_constants():
                dve.wait_ge(const_landed, N_CONST * DMA)
                dve.wait_ge(corner_zero, 1)
                nc.vector.tensor_copy(idb_sb[:], id_sb[:]).then_inc(const_set, 1)
                nc.vector.tensor_copy(corner_sb[:], corner_f[:].unsqueeze(1).broadcast_to([P, BLK, CORNER])).then_inc(const_set, 1)
                for qb in range(BLK):
                    nc.vector.tensor_copy(corner_rows[:, qb, qb * P + STEPS_T:(qb + 1) * P], corner_f[:]).then_inc(corner_laid, 1)
                dve.wait_ge(corner_laid, 2)

            def max_lo(b, hf):
                wait(dve, m_hi, b * 2 + hf + 1)
                nc.vector.tensor_tensor(mrow_lo[hf][:], ps_m[0][0:BLK * HALF, 0:P], mrow_hi[hf][:].bitcast(F32),
                                        ALU.subtract).then_inc(m_lo, 1)

            def normalise(b, qb):
                quad = ps_m[qb][:].rearrange("p (h c) -> p h c", c=VCOLS)
                wait(dve, o_turned, b * 2 + qb + 1)
                nc.vector.reciprocal(recip[:, qb, :], quad[:, :, DH]).then_inc(recip_done, 1)
                wait(dve, oT_done, b)
                wait(dve, recip_done, b * 2 + qb + 1)
                nc.vector.tensor_tensor(o_norm[:, qb, :].rearrange("p (h d) -> p h d", d=DH), quad[:, :, 0:DH],
                                        recip[:, qb, :].unsqueeze(2).broadcast_to([P, HEADS, DH]),
                                        ALU.mult).then_inc(normed, 1)

            def step(t, s):
                if isinstance(t, int) and t == BATCH:
                    dve.wait_ge(carried.x_hi, 1)
                    nc.vector.tensor_tensor(carried.x_parts[:, 1, :], ps_a[0][:], carried.x_parts[:, 0, :].bitcast(F32),
                                            ALU.subtract).then_inc(carried.x_lo, 1)
                    dve.wait_ge(lo_seen, N_PIECES)
                    nc.vector.tensor_scalar(has_lo[:], lo_max[:], 0.0, None, ALU.not_equal).then_inc(lo_marked, 1)
                for k in range(HEADS):
                    if live(t + 1, BATCH):
                        if k % HALF == 0:
                            wait(dve, mT_done, (t + 1) * 2 + k // HALF - 1)
                        wait(dve, max_done, (t + 1) * HEADS + k - 1)
                        wait_apart(dve, scores_a, (t + 1) * HEADS + k + 1, passed["dve"])
                        for qb in range(BLK):
                            ins = nc.vector.tensor_tensor_reduce(
                                scored[:, k % 2, qb, :], ps_a[A_BANK[k]][:, qb * SEQ:(qb + 1) * SEQ], corner_rows[:, qb, :], -1.0, F32_MAX,
                                ALU.add, ALU.min, negmax[:, k // HALF, k % HALF, qb:qb + 1])
                        ins.then_inc(max_done, 1)
                    if k == DVE_AT["max lo 1"] and live(t, BATCH):
                        max_lo(t, 1)
                    if k == DVE_AT["qk lo"] and live(t + 2, BATCH):
                        wait(dve, qk_hi, (t + 3) * 2)
                        nc.vector.scalar_tensor_tensor(
                            out=qk_sb[:, QL, :], in0=ps_m[0][:, 0:SEQ], scalar=qscale_sb[:, 0:1],
                            in1=qk_sb[:, QH, :].bitcast(F32), op0=ALU.mult, op1=ALU.subtract).then_inc(qk_lo, 1)
                        nc.vector.tensor_tensor(qk_sb[:, KL, :], ps_m[0][:, SEQ:2 * SEQ], qk_sb[:, KH, :].bitcast(F32),
                                                ALU.subtract).then_inc(qk_lo, 1)
                    if k in DVE_AT["norm"] and live(t - 1, BATCH):
                        normalise(t - 1, DVE_AT["norm"].index(k))
                    if k == DVE_AT["max lo 0"] and live(t + 1, BATCH):
                        max_lo(t + 1, 0)
                    if k == DVE_AT["res"] and live(t - 1, BATCH):
                        wait(dve, wo_done, t)
                        wait(dve, xb_done, t)
                        wait(dve, x1_done, t - 2)
                        r = res[1 - s]
                        nc.vector.tensor_tensor(r[:].rearrange("p a d -> p (a d)"), ps_m[1][:, 0:BLK * D],
                                                xb_sb[1 - s][:].rearrange("p a d -> p (a d)"), ALU.add).then_inc(res_done, 1)
                        wait(dve, res_done, t)
                        for a in range(BLK):
                            nc.vector.bn_stats(bn6[:, a, :], res[1 - s][:, a, :]).then_inc(bn_done, 1)
                    if k == DVE_AT["stats"] and live(t - 1, BATCH):
                        wait_apart(dve, bn_done, t * BLK, passed["dve"])
                        for a in range(BLK):
                            nc.vector.bn_aggr(meanvar[1 - s][:, a, :], bn6[:, a, :]).then_inc(stats_done, 1)
                    if isinstance(t, int):
                        for n in pieces_of(t, k - 1):
                            hi, lo, _ = pieces[n]
                            dve.wait_ge(raw_hi, n + 1)
                            nc.vector.tensor_tensor(lo, raw_piece(n), hi.bitcast(F32), ALU.subtract).then_inc(raw_split, 1)
                        for n in pieces_of(t, k - 3):
                            dve.wait_ge(raw_split, n + 1)
                            nc.vector.tensor_reduce(lo_max[:, n:n + 1], pieces[n][1].bitcast(F32), AX_XY, ALU.max,
                                                    apply_absolute_value=True).then_inc(lo_seen, 1)
                    if isinstance(t, int) and t == FIRST and k == 6:
                        lay_constants()
                    if isinstance(t, int) and t == FIRST and k == 15:
                        lay_rows(1)

            nc.vector.memset(corner_rows[:], 0.0).then_inc(corner_zero, 1)
            dve.wait_ge(rows_landed, DMA)
            lay_rows(0)
            drive(dve, step, **STEPS)
            dve.wait_ge(lo_counted, 1)
            nc.vector.tensor_reduce(carried.flag[:], ps_b[0][0:1, 0:N_PIECES], AX_X, ALU.max).then_inc(carried.flag_set, 1)

        @block.gpsimd
        def _(pool):
            for i in range(2):
                nc.gpsimd.memset(v_aug[i][:, :, :, DH + 1:VCOLS], 0.0).then_inc(v_laid, 1)
                nc.gpsimd.memset(v_aug[i][:, :, :, DH:DH + 1], 1.0).then_inc(v_laid, 1)
            nc.gpsimd.memset(carried.minus_half[:], -0.5).then_inc(carried.eps_done, 1)
            nc.gpsimd.memset(ones[:], 1.0).then_inc(ones_set, 1)
            bo_b = bo_sb[:].unsqueeze(1).broadcast_to([P, BLK, D])

            def step(t, s):
                if isinstance(t, int):
                    for n in pieces_of(t, None):
                        if n >= RAW_BUFS:
                            pool.wait_ge(raw_split, n - RAW_BUFS + 1)
                        nc.gpsimd.dma_start(raw_piece(n), pieces[n][2]).then_inc(raw_landed[n % RAW_BUFS], DMA)
                if live(t, BATCH):
                    if isinstance(t, int) and t == 0:
                        pool.wait_ge(const_landed, N_CONST * DMA)
                    wait(pool, x_landed, (t + 1) * DMA)
                    wait(pool, res_done, t - 1)
                    nc.gpsimd.tensor_tensor(xb_sb[s][:], x_sb[s][:], bo_b, ALU.add).then_inc(xb_done, 1)
                if live(t - 1, BATCH - 1):
                    norm_x1(nc, pool, t - 1, 1 - s, carried, passed["pool"])

            drive(pool, step, **STEPS)


def ffn(nc, wts, x1_dram, out, carried):
    (w1h, w1l), (w2h, w2l), (h1h, h1l), (h2h, h2l), (w3h, w3l) = wts
    with ExitStack() as ctx:
        def sb(name, shape, dt=F32):
            return ctx.enter_context(nc.sbuf_tensor(name, shape, dt))

        def sem(name):
            return ctx.enter_context(nc.semaphore(name))

        id_sb, minus_half, sc, sc3, x_in = carried.id_sb, carried.minus_half, carried.sc, carried.sc3, carried.x_in
        xh, xl = (carried.x_parts[:, i, :] for i in range(2))
        xin_landed, xT_done, x_hi, x_lo = carried.xin_landed, carried.xT_done, carried.x_hi, carried.x_lo
        x_res = sb("x_res", [P, CB, D])
        act_f = sb("act_f", [P, KT, CHUNK])
        gate_f = sb("gate_f", [P, KT, CHUNK])
        g1h, g1l = sb("g1h", [P, KT, CHUNK], F32R), sb("g1l", [P, KT, CHUNK], F32R)
        g2h, g2l = sb("g2h", [P, KT, CHUNK], F32R), sb("g2l", [P, KT, CHUNK], F32R)
        g3h, g3l = sb("g3h", [P, KT, CHUNK], F32R), sb("g3l", [P, KT, CHUNK], F32R)
        gelu_f = sb("gelu_f", [P, KT, CHUNK])
        y_sb = sb("y_sb", [P, CHUNK])
        res = sb("res_f", [P, CB, D])
        bn6 = sb("bn6_f", [P, CB, 6])
        meanvar = sb("meanvar_f", [P, CB, 2])
        vareps = sb("vareps_f", [P, CB])
        rstd = sb("rstd_f", [P, CB])
        y_out = sb("y_out", [P, CB, D])

        ps_r = [ctx.enter_context(nc.psum_tensor(f"ps_r{i}", [P, 512], F32)) for i in range(4)]
        ps_s = [ctx.enter_context(nc.psum_tensor(f"ps_s{i}", [P, 512], F32)) for i in range(2)]
        ps_y = ctx.enter_context(nc.psum_tensor("ps_y", [P, 512], F32))
        ps_x = ctx.enter_context(nc.psum_tensor("ps_x", [P, 512], F32))

        passed = {e: sem(f"passed2_{e}") for e in ("sp", "dve", "pool")}
        xres_landed, out_stored = sem("xres_landed"), sem("out_stored")
        silu_in, up_in, silu_done, gate_done = sem("silu_in"), sem("up_in"), sem("silu_done"), sem("gate_done")
        g1_hi, g1_lo = sem("g1_hi"), sem("g1_lo")
        l2_done, gelu2_done, g2_lo = sem("l2_done"), sem("gelu2_done"), sem("g2_lo")
        l3_done, gelu3_done, g3_lo = sem("l3_done"), sem("gelu3_done"), sem("g3_lo")
        l4_done, y_copied, y_turned = sem("l4_done"), sem("y_copied"), sem("y_turned")
        res_done, bn_done, stats_done = sem("res2_done"), sem("bn2_done"), sem("stats2_done")
        eps_done, rstd_done, out_done = sem("eps2_done"), sem("rstd2_done"), sem("out_done")

        STEPS = dict(first=-1, loop_from=3, loop_to=CHUNKS - 3, last=CHUNKS, unroll=1)

        block = ctx.enter_context(nc.Block())

        def tokens(dram, c):
            return dram[c].rearrange("a p d -> p a d")

        out_c = out.rearrange("(c n) (a p) d -> c p n a d", n=CHUNK // SEQ, p=P)
        NB = CHUNK // SEQ

        @block.sync
        def _(sp):
            def step(c, s):
                if live(c - 1, CHUNKS):
                    wait_apart(sp, res_done, c - 1, passed["sp"])
                    load_chunk(sp, x1_dram, c - 1, x_res, xres_landed)
                if live(c - 2, CHUNKS):
                    wait_apart(sp, out_done, c - 1, passed["sp"])
                    for n in range(NB):
                        sp.dma_start(out_c[c - 2, :, n, :, :], y_out[:, n * BLK:(n + 1) * BLK, :]).then_inc(out_stored, DMA)
                if live(c + 3, CHUNKS):
                    wait_apart(sp, xT_done, c + 3, passed["sp"])
                    load_chunk(sp, x1_dram, c + 3, x_in, xin_landed)
                if isinstance(c, int) and c == 0:
                    sp.wait_ge(carried.x1_done, BATCH)
                    sp.dma_start(x1_dram[BATCH - 1], carried.x1_sb[(BATCH - 1) % 2][:]).then_inc(carried.x1_stored, DMA)
                if isinstance(c, int) and c == 1:
                    sp.wait_ge(carried.x1_stored, BATCH * DMA)

            drive(sp, step, **STEPS)
            sp.wait_ge(out_done, CHUNKS)
            for n in range(NB):
                sp.dma_start(out_c[CHUNKS - 1, :, n, :, :], y_out[:, n * BLK:(n + 1) * BLK, :]).then_inc(out_stored, DMA)
            sp.wait_ge(out_stored, CHUNKS * NB * DMA)

        @block.tensor
        def _(pe):
            def product(ps, o, wh, wl, ah, al, kt, ready=None):
                for k in range(kt):
                    if ready is not None:
                        ready(k)
                    w_hi = wh[:, k, o * P:(o + 1) * P]
                    a_hi, a_lo = (ah[:, k, :], al[:, k, :]) if kt > 1 else (ah, al)
                    pe.matmul(ps[:], w_hi, a_hi, start=(k == 0), stop=False)
                    if wl is not None:
                        pe.matmul(ps[:], wl[:, k, o * P:(o + 1) * P], a_hi, start=False, stop=False)
                    mm = pe.matmul(ps[:], w_hi, a_lo, start=False, stop=(k == kt - 1))
                return mm

            def step(c, s, lows):
                if live(c, CHUNKS):
                    for o in range(KT):
                        wait(pe, gelu3_done, (c - 1) * KT + o + 1)
                        ready = (lambda k: wait(pe, g1_lo, c * KT + k + 1)) if o == 0 else None
                        product(ps_r[o], o, h1h, lows["h1"], g1h, g1l, KT, ready).then_inc(l2_done, 1)
                if live(c - 1, CHUNKS):
                    wait(pe, res_done, c - 1)
                    product(ps_y, 0, w3h, lows["w3"], g3h, g3l, KT,
                            lambda k: wait(pe, g3_lo, (c - 1) * KT + k + 1)).then_inc(l4_done, 1)
                if live(c + 1, CHUNKS):
                    wait(pe, x_lo, c + 2)
                    for o in range(KT):
                        wait(pe, silu_done, (c + 1) * KT + o - 1)
                        product(ps_s[o % 2], o, w1h, lows["w1"], xh, xl, 1).then_inc(silu_in, 1)
                        if live(c, CHUNKS):
                            wait(pe, gelu2_done, c * KT + o + 1)
                        product(ps_r[o], o, w2h, lows["w2"], xh, xl, 1).then_inc(up_in, 1)
                if live(c + 2, CHUNKS):
                    wait(pe, xin_landed, (c + 3) * NB * DMA)
                    wait(pe, x_lo, c + 2)
                    for a in range(CB):
                        mm = pe.transpose(ps_x[:, a * P:(a + 1) * P], x_in[:, a, :], id_sb[:])
                    mm.then_inc(xT_done, 1)
                if live(c - 1, CHUNKS):
                    wait(pe, y_copied, c)
                    for a in range(CB):
                        mm = pe.transpose(ps_y[:, a * P:(a + 1) * P], y_sb[:, a * P:(a + 1) * P], id_sb[:])
                    mm.then_inc(y_turned, 1)
                if live(c, CHUNKS):
                    for o in range(KT):
                        if live(c + 1, CHUNKS):
                            wait(pe, gate_done, (c + 1) * KT + o + 1)
                        else:
                            wait(pe, gelu2_done, c * KT + o + 1)
                        ready = (lambda k: wait(pe, g2_lo, c * KT + k + 1)) if o == 0 else None
                        product(ps_r[o], o, h2h, lows["h2"], g2h, g2l, KT, ready).then_inc(l3_done, 1)

            pe.wait_ge(carried.flag_set, 1)
            any_lo = pe.value_load(carried.flag[:].bitcast(mybir.dt.int32))
            weight_lows = {"w1": w1l, "w2": w2l, "h1": h1l, "h2": h2l, "w3": w3l}
            with pe.If(any_lo != 0):
                drive(pe, lambda c, s: step(c, s, weight_lows), **STEPS)
            with pe.Else():
                drive(pe, lambda c, s: step(c, s, dict.fromkeys(weight_lows)), **STEPS)

        @block.scalar
        def _(act):
            def gelus(c, layer, in_done, out_hi, prev_use, prev_lo, done):
                for o in range(KT):
                    wait(act, in_done, c * KT + o + 1)
                    wait(act, prev_lo[0], prev_lo[1] + o + 1)
                    if o == 0 and prev_use is not None:
                        wait(act, *prev_use)
                    scale = sc[:, 2 + layer, o:o + 1]
                    nc.scalar.activation(gelu_f[:, o, :], ps_r[o][:], ACT.Gelu, scale=scale)
                    nc.scalar.activation(out_hi[:, o, :], ps_r[o][:], ACT.Gelu, scale=scale).then_inc(done, 1)

            def step(c, s):
                if live(c, CHUNKS):
                    gelus(c, 0, l2_done, g2h, (l3_done, c * KT), (g3_lo, (c - 1) * KT), gelu2_done)
                for o in range(KT):
                    if live(c + 1, CHUNKS):
                        wait(act, silu_in, (c + 1) * KT + o + 1)
                        wait(act, gate_done, c * KT + o + 1)
                        nc.scalar.activation(act_f[:, o, :], ps_s[o % 2][:], ACT.Silu,
                                             scale=sc[:, 0, o:o + 1]).then_inc(silu_done, 1)
                    if o == 1 and live(c - 1, CHUNKS):
                        wait(act, l4_done, c)
                        wait(act, y_turned, c - 1)
                        nc.scalar.activation(y_sb[:], ps_y[:], ACT.Copy, scale=sc3[:, 0:1]).then_inc(y_copied, 1)
                if live(c + 2, CHUNKS):
                    wait(act, xT_done, c + 3)
                    wait(act, up_in, (c + 2) * KT)
                    nc.scalar.activation(xh, ps_x[:], ACT.Copy).then_inc(x_hi, 1)
                if live(c, CHUNKS):
                    gelus(c, 1, l3_done, g3h, (l4_done, c), (g2_lo, c * KT), gelu3_done)

            act.wait_ge(carried.scales_landed, 5 * DMA)
            drive(act, step, **STEPS)

        @block.vector
        def _(dve):
            def lows(c, hi, lo, done, signal):
                for o in range(KT):
                    wait(dve, done, c * KT + o + 1)
                    nc.vector.tensor_tensor(lo[:, o, :], gelu_f[:, o, :], hi[:, o, :].bitcast(F32),
                                            ALU.subtract).then_inc(signal, 1)

            def normalise(c):
                wait(dve, rstd_done, c + 1)
                wait(dve, out_stored, c * NB * DMA)
                wait_apart(dve, stats_done, (c + 1) * CB, passed["dve"])
                for a in range(CB):
                    ins = nc.vector.tensor_scalar(y_out[:, a, :], res[:, a, :], meanvar[:, a, 0:1],
                                                  rstd[:, a:a + 1], ALU.subtract, ALU.mult)
                ins.then_inc(out_done, 1)

            def step(c, s):
                if live(c, CHUNKS):
                    lows(c, g2h, g2l, gelu2_done, g2_lo)
                if live(c - 2, CHUNKS):
                    normalise(c - 2)
                if live(c + 1, CHUNKS):
                    wait(dve, l2_done, (c + 1) * KT)
                    for o in range(KT):
                        n = (c + 1) * KT + o + 1
                        wait(dve, silu_done, n)
                        wait(dve, up_in, n)
                        wait(dve, g1_lo, c * KT + o + 1)
                        nc.vector.scalar_tensor_tensor(out=gate_f[:, o, :], in0=ps_r[o][:], scalar=sc[:, 1, o:o + 1],
                                                       in1=act_f[:, o, :], op0=ALU.mult,
                                                       op1=ALU.mult).then_inc(gate_done, 1)
                    for i in range(KT + 1):
                        n = (c + 1) * KT + i
                        if i < KT:
                            wait(dve, gate_done, n + 1)
                            nc.vector.tensor_copy(g1h[:, i, :], gate_f[:, i, :]).then_inc(g1_hi, 1)
                        if i > 0:
                            wait(dve, g1_hi, n)
                            nc.vector.tensor_tensor(g1l[:, i - 1, :], gate_f[:, i - 1, :], g1h[:, i - 1, :].bitcast(F32),
                                                    ALU.subtract).then_inc(g1_lo, 1)
                if live(c + 2, CHUNKS):
                    wait(dve, x_hi, c + 3)
                    nc.vector.tensor_tensor(xl, ps_x[:], xh.bitcast(F32), ALU.subtract).then_inc(x_lo, 1)
                if live(c - 1, CHUNKS):
                    wait(dve, y_turned, c)
                    wait(dve, xres_landed, c * NB * DMA)
                    wait(dve, out_done, c - 1)
                    nc.vector.tensor_tensor(res[:].rearrange("p a d -> p (a d)"), ps_y[:],
                                            x_res[:].rearrange("p a d -> p (a d)"), ALU.add).then_inc(res_done, 1)
                if live(c, CHUNKS):
                    lows(c, g3h, g3l, gelu3_done, g3_lo)
                if live(c - 1, CHUNKS):
                    wait(dve, res_done, c)
                    for a in range(CB):
                        nc.vector.bn_stats(bn6[:, a, :], res[:, a, :]).then_inc(bn_done, 1)
                    wait_apart(dve, bn_done, c * CB, passed["dve"])
                    for a in range(CB):
                        nc.vector.bn_aggr(meanvar[:, a, :], bn6[:, a, :]).then_inc(stats_done, 1)

            dve.wait_ge(carried.scales_landed, 5 * DMA)
            drive(dve, step, **STEPS)
            normalise(CHUNKS - 1)

        @block.gpsimd
        def _(pool):
            norm_x1(nc, pool, BATCH - 1, (BATCH - 1) % 2, carried, passed["pool"])

            def step(c, s):
                if live(c - 1, CHUNKS):
                    wait(pool, out_done, c - 1)
                    wait_apart(pool, stats_done, c * CB, passed["pool"])
                    nc.gpsimd.tensor_scalar(vareps[:], meanvar[:, :, 1], EPS, None, ALU.add).then_inc(eps_done, 1)
                    wait(pool, eps_done, c)
                    nc.gpsimd.tensor_tensor(rstd[:], vareps[:], minus_half[:], ALU.pow).then_inc(rstd_done, 1)

            drive(pool, step, **STEPS)


def build(nc, a, out):
    x1_dram = nc.dram_tensor("x1_scratch", [BATCH, P, BLK, D], F32, kind="Internal").ap()
    qk_dram = nc.dram_tensor("qk_scratch", [2, 2, 3, DH, HEADS, SEQ], F32, kind="Internal").ap()
    with ExitStack() as ctx:
        wts = []
        for name, kt, n in (("w1", 1, HID), ("w2", 1, HID), ("h1", KT, HID), ("h2", KT, HID), ("w3", KT, D)):
            wts.append(tuple(ctx.enter_context(nc.sbuf_tensor(f"{name}_{part}", [P, kt, n], F32R)) for part in ("hi", "lo")))
        scales = [a[n] for n in ("w1_s", "w2_s", "h1_s", "h2_s", "w3_s")]
        carried = Carried(nc, ctx)
        raw_w = [a[n].rearrange("(k p) n -> p k n", p=P) for n in ("w1T", "w2T", "h1T", "h2T", "w3T")]
        attention(nc, wts, a["x"], a["xT"], a["wqT"], a["wkT"], a["wvT"], a["woT"], a["bo"], a["qscale"], a["ident"],
                  a["corner"], a["rows"], x1_dram, qk_dram, raw_w, scales, carried)
        ffn(nc, wts, x1_dram, out, carried)


def bias_rows():
    pos = np.arange(SEQ, dtype=np.float32)
    local = pos % P
    first = (pos < P).astype(np.float32)
    second = 1.0 - first
    sign = first - second
    one = np.ones_like(pos)
    pairs = [(sign * pos, one), (-sign, pos), (-2.0 * pos * first, first), (second, -2.0 * local * second)]
    for block in (first, second):
        for t in range(1, STEPS_T + 1):
            pairs.append((block * (local >= t), 2.0 * block * (local >= t)))
    rows = np.zeros((P, 2, SEQ), np.float32)
    for r, (query, key) in enumerate(pairs):
        rows[STACK + r, 0], rows[STACK + r, 1] = query, key
    rows[MROW:, 1] = 1.0
    return rows


def shape_constants():
    i = np.arange(CORNER, dtype=np.float32)
    corner = np.zeros((P, CORNER), np.float32)
    corner[STEPS_T:, :] = 2.0 * np.minimum(i[:, None], i[None, :])
    qscale = np.tile(1.0 / (np.array(slopes()) * np.sqrt(float(DH))), DH).astype(np.float32)
    return {
        "qscale": qscale.reshape(P, 1),
        "ident": np.eye(P, dtype=np.float32),
        "corner": corner,
        "rows": bias_rows(),
    }


def by_feature(w):
    return w.reshape(HEADS, DH, D).transpose(1, 0, 2).reshape(D, D).T


def kernel(**inputs):
    import concourse.bacc as bacc
    from concourse.bass_utils import run_bass_kernel_spmd

    x = inputs["L0_attn_x"]
    laid = {
        "x": x, "xT": x.transpose(0, 2, 1),
        "wqT": by_feature(inputs["L0_attn_wq"]), "wkT": by_feature(inputs["L0_attn_wk"]), "wvT": inputs["L0_attn_wv"].T,
        "woT": inputs["L0_attn_wo"].T, "bo": np.broadcast_to(inputs["L0_attn_bo"], (P, D)),
        "w1T": inputs["L0_ffn_w1_w"].T, "w2T": inputs["L0_ffn_w2_w"].T, "h1T": inputs["L0_ffn_h1_w"].T,
        "h2T": inputs["L0_ffn_h2_w"].T, "w3T": inputs["L0_ffn_w3_w"].T,
        **{f"{n}_s": inputs[f"L0_ffn_{n}_s"].reshape(-1, P).T for n in ("w1", "w2", "h1", "h2", "w3")},
        **shape_constants(),
    }
    nc = bacc.Bacc("TRN2", target_bir_lowering=False, num_devices=1)
    arrays, operands = {}, {}
    for name, value in laid.items():
        value = np.ascontiguousarray(value)
        arrays[f"in_{name}"] = value
        operands[name] = nc.dram_tensor(f"in_{name}", value.shape, mybir.dt.from_np(value.dtype), kind="ExternalInput").ap()
    out = nc.dram_tensor("out_0", (BATCH, SEQ, D), F32, kind="ExternalOutput").ap()
    build(nc, operands, out)
    r = run_bass_kernel_spmd(nc, [arrays], core_ids=[0])
    return r.results[0]["out_0"]
```
